# Optimizing a Trainium2 kernel written in Bass

```python
import numpy as np
import jax
import jax.numpy as jnp

def _softmax(x, axis=-1):
    return jax.nn.softmax(x, axis=axis)

def _gelu(x):
    return jax.nn.gelu(x, approximate=True)

def _silu(x):
    return jax.nn.silu(x)

def _sigmoid(x):
    return jax.nn.sigmoid(x)

def _layernorm(x, axis=-1, eps=1e-05):
    m = jnp.mean(x, axis=axis, keepdims=True)
    v = jnp.var(x, axis=axis, keepdims=True)
    return (x - m) / jnp.sqrt(v + eps)

def _scatter_add(tgt, idx, src, axis=0):
    return tgt.at[idx].add(src)

def _segment_sum(src, seg, n):
    return jax.ops.segment_sum(src, seg, n)
kernel_name = 'mk_xattn_ffn_d1_seqx_r8_18c863'

def setup_inputs(seed: int=0):
    np.random.seed(seed)
    _w = jnp.asarray

    def _rec_inputs():
        import jax
        import jax.numpy as jnp
        _rk = jax.random.key(seed)
        x = 7.22e-05 + 1 * jax.random.normal(jax.random.fold_in(_rk, 1), (8, 128, 512), jnp.float32)
        _lenS = 128 - jax.random.randint(jax.random.fold_in(_rk, 7), (8,), 0, max(1, 128 // 4) + 1, jnp.int32)
        _lenS2 = 128 - jax.random.randint(jax.random.fold_in(_rk, 8), (8,), 0, max(1, 128 // 4) + 1, jnp.int32)
        _ctx_4096P = jax.random.normal(jax.random.fold_in(_rk, 11), (8, 16, 512), jnp.float32)
        _ctx_4096c = jax.random.dirichlet(jax.random.fold_in(_rk, 511), 0.3 * jnp.ones((16,), jnp.float32), (8, 128))
        _ctx_4096t = jnp.einsum('bsk,bkd->bsd', _ctx_4096c, _ctx_4096P)
        _ctx_4096t = _ctx_4096t * jax.lax.rsqrt(jnp.mean(jnp.square(_ctx_4096t)) + 1e-12) * 0.953939
        ctx_4096 = 4.13588e-05 + 0.999923 * (_ctx_4096t + 0.3 * jax.random.normal(jax.random.fold_in(_rk, 611), (8, 128, 512), jnp.float32))
        _validS = jnp.arange(128)[None, :] < _lenS[:, None]
        _validS2 = jnp.arange(128)[None, :] < _lenS2[:, None]
        _causal = jnp.tril(jnp.ones((128, 128), dtype=bool))
        mask_1x1xSxS2_bk0 = jnp.logical_not(jnp.broadcast_to(_validS2[0:1, None, None, :], (1, 1, 128, 128)))
        return (x, ctx_4096, mask_1x1xSxS2_bk0)
    x, ctx_4096, mask_1x1xSxS2_bk0 = _rec_inputs()

    def _L0_xattn_setup():
        import jax, jax.numpy as jnp
        import numpy as np
        B, T, D_MODEL = (1, 256, 512)
        NUM_Q_HEADS, NUM_KV_HEADS, KEY_SIZE = (32, 8, 128)
        ATTN_MULT = 0.08838834764831845
        MAX_ATTN_VAL = 30.0

        def rotate_half(x):
            x1, x2 = jnp.split(x, 2, axis=-1)
            return jnp.concatenate((-x2, x1), axis=-1)

        def apply_rope(x):
            b, t, h, d = x.shape
            exponents = jnp.arange(0, d, 2, dtype=jnp.float32)
            inv_freq = 1.0 / 10000.0 ** (exponents / d)
            pos = jnp.arange(t, dtype=jnp.float32)
            phase = pos[:, None] * inv_freq[None, :]
            phase = jnp.tile(phase, (1, 2))[None, :, None, :]
            return (x * jnp.cos(phase) + rotate_half(x) * jnp.sin(phase)).astype(x.dtype)
        key = jax.random.key(seed)
        ks = jax.random.split(key, 8)
        query = jax.random.normal(ks[0], (B, T, D_MODEL), dtype=jnp.float32)
        kk = jax.random.normal(ks[1], (B, T, D_MODEL), dtype=jnp.float32)
        vv = jax.random.normal(ks[2], (B, T, D_MODEL), dtype=jnp.float32)
        mask = jnp.tril(jnp.ones((T, T), dtype=bool))[None, None, :, :]
        s = 0.02
        Wq = jax.random.normal(ks[3], (D_MODEL, NUM_Q_HEADS * KEY_SIZE), dtype=jnp.float32) * s
        Wk = jax.random.normal(ks[4], (D_MODEL, NUM_KV_HEADS * KEY_SIZE), dtype=jnp.float32) * s
        Wv = jax.random.normal(ks[5], (D_MODEL, NUM_KV_HEADS * KEY_SIZE), dtype=jnp.float32) * s
        Wo = jax.random.normal(ks[6], (NUM_Q_HEADS * KEY_SIZE, D_MODEL), dtype=jnp.float32) * s
        return {'query': query, 'key': kk, 'value': vv, 'mask': mask, 'Wq': Wq, 'Wk': Wk, 'Wv': Wv, 'Wo': Wo}
    _L0_xattn_all = _L0_xattn_setup()
    _L0_xattn_in = {k: v for k, v in _L0_xattn_all.items() if k in ('Wq', 'Wk', 'Wv', 'Wo')}
    del _L0_xattn_all

    def _L0_ffn_setup():
        import jax, jax.numpy as jnp
        import numpy as np
        NF4_CODE = jnp.array([-1.0, -0.6961928009986877, -0.5250730514526367, -0.39491748809814453, -0.28444138169288635, -0.18477343022823334, -0.09105003625154495, 0.0, 0.07958029955625534, 0.16093020141124725, 0.24611230194568634, 0.33791524171829224, 0.44070982933044434, 0.5626170039176941, 0.7229568362236023, 1.0], dtype=jnp.float32)
        BLOCKSIZE = 64

        def nf4_quant_dequant(w):
            shape = w.shape
            flat = w.reshape(-1, BLOCKSIZE)
            absmax = jnp.max(jnp.abs(flat), axis=1, keepdims=True)
            normalized = flat / jnp.where(absmax == 0, 1.0, absmax)
            bounds = (NF4_CODE[:-1] + NF4_CODE[1:]) * 0.5
            idx = jnp.searchsorted(bounds, normalized)
            return (NF4_CODE[idx] * absmax).reshape(shape)
        key = jax.random.key(seed)
        k1, k2, k3, kx = jax.random.split(key, 4)
        D, H = (512, 1376)
        scale = 0.02
        w1 = jax.random.normal(k1, (H, D), jnp.float32) * scale
        w2 = jax.random.normal(k2, (H, D), jnp.float32) * scale
        w3 = jax.random.normal(k3, (D, H), jnp.float32) * scale
        x = jax.random.normal(kx, (2, 256, D), jnp.float32)
        return {'x': x, 'w1': w1, 'w2': w2, 'w3': w3}
    _L0_ffn_all = _L0_ffn_setup()
    _L0_ffn_in = {k: v for k, v in _L0_ffn_all.items() if k in ('w1', 'w2', 'w3')}
    del _L0_ffn_all
    return {'x': x, 'ctx_4096': ctx_4096, 'mask_1x1xSxS2_bk0': mask_1x1xSxS2_bk0, 'L0_xattn_Wq': _L0_xattn_in['Wq'], 'L0_xattn_Wk': _L0_xattn_in['Wk'], 'L0_xattn_Wv': _L0_xattn_in['Wv'], 'L0_xattn_Wo': _L0_xattn_in['Wo'], 'L0_ffn_w1': _L0_ffn_in['w1'], 'L0_ffn_w2': _L0_ffn_in['w2'], 'L0_ffn_w3': _L0_ffn_in['w3']}

def reference(x, ctx_4096, mask_1x1xSxS2_bk0, L0_xattn_Wq, L0_xattn_Wk, L0_xattn_Wv, L0_xattn_Wo, L0_ffn_w1, L0_ffn_w2, L0_ffn_w3):
    import jax
    import jax.numpy as jnp

    def _L0_xattn_ref(query, key, value, mask, Wq, Wk, Wv, Wo):
        import jax, jax.numpy as jnp
        import numpy as np
        B, T, D_MODEL = (1, 256, 512)
        NUM_Q_HEADS, NUM_KV_HEADS, KEY_SIZE = (32, 8, 128)
        ATTN_MULT = 0.08838834764831845
        MAX_ATTN_VAL = 30.0

        def rotate_half(x):
            x1, x2 = jnp.split(x, 2, axis=-1)
            return jnp.concatenate((-x2, x1), axis=-1)

        def apply_rope(x):
            b, t, h, d = x.shape
            exponents = jnp.arange(0, d, 2, dtype=jnp.float32)
            inv_freq = 1.0 / 10000.0 ** (exponents / d)
            pos = jnp.arange(t, dtype=jnp.float32)
            phase = pos[:, None] * inv_freq[None, :]
            phase = jnp.tile(phase, (1, 2))[None, :, None, :]
            return (x * jnp.cos(phase) + rotate_half(x) * jnp.sin(phase)).astype(x.dtype)
        b, t, _ = query.shape
        d = KEY_SIZE
        h, kv_h = (NUM_Q_HEADS, NUM_KV_HEADS)
        g = h // kv_h
        q = (query @ Wq).reshape(b, t, h, d)
        k = (key @ Wk).reshape(b, t, kv_h, d)
        v = (value @ Wv).reshape(b, t, kv_h, d)
        q = apply_rope(q)
        k = apply_rope(k)
        q = q.reshape(b, t, kv_h, g, d)
        logits = jnp.einsum('btkgd,bTkd->bkgtT', q, k).astype(jnp.float32)
        logits = logits * ATTN_MULT
        logits = MAX_ATTN_VAL * jnp.tanh(logits / MAX_ATTN_VAL)
        m = mask[:, :, None, :, :]
        logits = jnp.where(m, logits, -1e+30)
        weights = jax.nn.softmax(logits, axis=-1).astype(query.dtype)
        attn = jnp.einsum('bkgtT,bTkd->btkgd', weights, v)
        attn = attn.reshape(b, t, h * d)
        return attn @ Wo

    def _L0_ffn_ref(x, w1, w2, w3):
        import jax, jax.numpy as jnp
        import numpy as np
        NF4_CODE = jnp.array([-1.0, -0.6961928009986877, -0.5250730514526367, -0.39491748809814453, -0.28444138169288635, -0.18477343022823334, -0.09105003625154495, 0.0, 0.07958029955625534, 0.16093020141124725, 0.24611230194568634, 0.33791524171829224, 0.44070982933044434, 0.5626170039176941, 0.7229568362236023, 1.0], dtype=jnp.float32)
        BLOCKSIZE = 64

        def nf4_quant_dequant(w):
            shape = w.shape
            flat = w.reshape(-1, BLOCKSIZE)
            absmax = jnp.max(jnp.abs(flat), axis=1, keepdims=True)
            normalized = flat / jnp.where(absmax == 0, 1.0, absmax)
            bounds = (NF4_CODE[:-1] + NF4_CODE[1:]) * 0.5
            idx = jnp.searchsorted(bounds, normalized)
            return (NF4_CODE[idx] * absmax).reshape(shape)
        dq1 = nf4_quant_dequant(w1)
        dq2 = nf4_quant_dequant(w2)
        dq3 = nf4_quant_dequant(w3)
        gate = jnp.einsum('bsd,hd->bsh', x, dq1)
        up = jnp.einsum('bsd,hd->bsh', x, dq2)
        h = jax.nn.silu(gate) * up
        return jnp.einsum('bsh,dh->bsd', h, dq3)
    x = x + _L0_xattn_ref(_layernorm(x, axis=-1), ctx_4096, ctx_4096, mask_1x1xSxS2_bk0, L0_xattn_Wq, L0_xattn_Wk, L0_xattn_Wv, L0_xattn_Wo)
    x = x + _L0_ffn_ref(_layernorm(x, axis=-1), L0_ffn_w1, L0_ffn_w2, L0_ffn_w3)
    return x

_drawn_inputs = setup_inputs


def setup_inputs(seed=0):
    import zlib

    import numpy as np

    out = dict(_drawn_inputs(seed))
    spreads = {}
    factors = {}
    for name, (base, spread) in spreads.items():
        noise = np.random.default_rng([zlib.crc32(name.encode()), seed]).standard_normal(out[name].shape)
        drawn = base * np.exp(spread * noise) if base else spread * noise
        out[name] = jnp.asarray(drawn.astype(out[name].dtype))
    for name, factor in factors.items():
        out[name] = (out[name] * factor).astype(out[name].dtype)
    return out
```

```python
import numpy as np
import concourse.bass as bass
import concourse.mybir as mybir

B, S, D = 8, 128, 512
TOK = B * S
KT = D // 128
NKV, G, DH = 8, 4, 128
NQ = NKV * G
HID = 1376
HT = -(-HID // 128)
HLAST = HID - 128 * (HT - 1)
BLK = 64
NFW = 11 * D
CH = 22 * BLK
NCHUNK = 3 * NFW // CH
MULT, CAP = 0.08838834764831845, 30.0
EPS = 1e-5

NF4_CODE = [-1.0, -0.6961928009986877, -0.5250730514526367, -0.39491748809814453, -0.28444138169288635,
            -0.18477343022823334, -0.09105003625154495, 0.0, 0.07958029955625534, 0.16093020141124725,
            0.24611230194568634, 0.33791524171829224, 0.44070982933044434, 0.5626170039176941,
            0.7229568362236023, 1.0]


def nf4_constants():
    code = np.array(NF4_CODE, np.float32)
    bounds = (code[:-1] + code[1:]) * np.float32(0.5)
    steps = []
    for i in range(15):
        d = np.float32(code[i + 1] - code[i])
        for c in (d, np.nextafter(d, np.float32(9)), np.nextafter(d, np.float32(-9))):
            if np.float32(code[i] + c) == code[i + 1]:
                steps.append(float(c))
                break
    assert len(steps) == 15
    return [float(b) for b in bounds], steps


def build(nc, x_d, ctx_t, wk_d, wv_d, wq_d, wo_d, nf_d, mask_t, table_d, out_d):
    from contextlib import ExitStack
    f32, f32r, u8 = mybir.dt.float32, mybir.dt.float32r, mybir.dt.uint8
    ALU, ACT, AX = mybir.AluOpType, mybir.ActivationFunctionType, mybir.AxisListType
    BOUNDS, STEPS = nf4_constants()
    ctx = ExitStack()
    with ctx:
        def sem(name):
            return ctx.enter_context(nc.semaphore(name))

        def sb(name, shape, dt=f32, where=ctx):
            return where.enter_context(nc.sbuf_tensor(name, shape, dt))

        y = sb("y", [128, B, D])
        tab = sb("tab", [128, 3, 128])
        mt8 = sb("mt8", [128, S], u8)
        maskf = sb("maskf", [128, S])
        nomask = sb("nomask", [128, S])
        keep = sb("keep", [128, S])
        cosq = sb("cosq", [128, S])
        sinq = sb("sinq", [128, S])
        ones = sb("ones", [128, 128])
        stat = sb("stat", [128, B, 6])
        bnd = sb("bnd", [128, 15])
        mv = sb("mv", [128, B, 2])
        veps = sb("veps", [128, B])
        std = sb("std", [128, B])
        rstd = sb("rstd", [128, B])
        nfv = sb("nfv", [128, CH])
        nfa = sb("nfa", [128, CH])
        nfp = sb("nfp", [128, 2, CH], u8)
        nfm = sb("nfm", [128, CH // BLK])
        nfg = sb("nfg", [128, CH // BLK])
        nfr = sb("nfr", [128, CH // BLK])
        stage = sb("stage", [128, 4, 512])
        nrm = sb("nrm", [128, 2, D])
        rs = sb("rs", [128, 4])

        with ExitStack() as down:
            w3h = sb("w3h", [128, HT, D], f32r, down)
            w3l = sb("w3l", [128, HT, D], f32r, down)
        xh = sb("xh", [128, KT, TOK], f32r)
        xl = sb("xl", [128, KT, TOK], f32r)
        with ExitStack() as ffn:
            wgh = sb("wgh", [128, 2, 2, KT, 128], f32r, ffn)
            wgl = sb("wgl", [128, 2, 2, KT, 128], f32r, ffn)
            sg = sb("sg", [128, 2, 512], f32, ffn)
            hf = sb("hf", [128, 2, 512], f32, ffn)
            hh = sb("hh", [128, HT, TOK], f32r, ffn)
            hl = sb("hl", [128, HT, TOK], f32r, ffn)
        kcur = sb("kcur", [128, 2, 512])
        vcur = sb("vcur", [128, B, DH + 1])
        sw = sb("sw", [128, 2, 512])
        eb = sb("eb", [128, 2, 512])
        qT = sb("qT", [128, 2, G, 512])
        wqh = sb("wqh", [128, G, KT, 128], f32r)
        wql = sb("wql", [128, G, KT, 128], f32r)
        with ExitStack() as kv_phase:
            wch0 = sb("wch0", [128, KT, 512], f32r, kv_phase)
            wcl0 = sb("wcl0", [128, KT, 512], f32r, kv_phase)
            wch1 = sb("wch1", [128, KT, 512], f32r, kv_phase)
            wcl1 = sb("wcl1", [128, KT, 512], f32r, kv_phase)
        wch, wcl = [wch0, wch1], [wcl0, wcl1]
        woh = sb("woh", [128, G, D], f32r)
        wol = sb("wol", [128, G, D], f32r)
        ath = sb("ath", [128, 4, 512], f32r)
        atl = sb("atl", [128, 4, 512], f32r)
        cth = sb("cth", [128, KT, TOK], f32r)
        ctl = sb("ctl", [128, KT, TOK], f32r)
        vst = sb("vst", [128, 4, 512])

        ks_d = nc.dram_tensor("ks_scratch", (NKV, 2, 128, 512), f32, kind="Internal").ap()
        vs_d = nc.dram_tensor("vs_scratch", (NKV, 2, 128, B // 2, DH), f32, kind="Internal").ap()
        dq12 = nc.dram_tensor("dq12_scratch", (128, 2 * NFW), f32, kind="Internal").ap()
        dq3 = nc.dram_tensor("dq3_scratch", (128, NFW), f32, kind="Internal").ap()

        bank = [ctx.enter_context(nc.psum_tensor(f"bank{i}", [128, 512], f32)) for i in range(5)]
        avp = ctx.enter_context(nc.psum_tensor("avp", [128, 2, 512], f32))
        trp = ctx.enter_context(nc.psum_tensor("trp", [128, 512], f32))
        prj, prj2, lgp = [bank[0], bank[1]], [bank[2], bank[3]], bank[4]
        trg = [trp, lgp]

        tab_in, mask_in, x_in = sem("tab_in"), sem("mask_in"), sem("x_in")
        piece_in = [sem(f"piece_in{i}") for i in range(4)]
        piece_hi, piece_lo = sem("piece_hi"), sem("piece_lo")
        k_out = [sem(f"k_out{i}") for i in range(8)]
        v_out = [sem(f"v_out{i}") for i in range(4)]
        k_in = [sem("k_in0"), sem("k_in1")]
        v_in = [sem("v_in0"), sem("v_in1")]
        nf_in, nf_step, nf_above, nf_out = sem("nf_in"), sem("nf_step"), sem("nf_above"), sem("nf_out")
        consts, masks, mask_count = sem("consts"), sem("masks"), sem("mask_count")
        ln_stat, ln_std, ln_rstd = sem("ln_stat"), sem("ln_std"), sem("ln_rstd")
        xn_done, xt_done, xt_hi, xt_lo = sem("xn_done"), sem("xt_done"), sem("xt_hi"), sem("xt_lo")
        proj_done, swapped, cos_done, sin_done, roped = (sem("proj_done"), sem("swapped"), sem("cos_done"),
                                                         sem("sin_done"), sem("roped"))
        vproj_done, v_copied = sem("vproj_done"), sem("v_copied")
        logits_done, tanh_done, exp_done, weights_done = (sem("logits_done"), sem("tanh_done"), sem("exp_done"),
                                                          sem("weights_done"))
        av_done, recip_done, an_done = sem("av_done"), sem("recip_done"), sem("an_done")
        at_done, at_hi, at_lo = sem("at_done"), sem("at_hi"), sem("at_lo")
        out_done, y_done = sem("out_done"), sem("y_done")
        wt_done, wt_hi, wt_lo = sem("wt_done"), sem("wt_hi"), sem("wt_lo")
        gate_done, silu_done, h_done, h_hi, h_lo = (sem("gate_done"), sem("silu_done"), sem("h_done"), sem("h_hi"),
                                                    sem("h_lo"))
        mask_step, stat_step = sem("mask_step"), sem("stat_step")
        down_done, final_done, stored = sem("down_done"), sem("final_done"), sem("stored")
        block = ctx.enter_context(nc.Block())

        def wait(eng, what, value):
            if not isinstance(value, int) or value > 0:
                eng.wait_ge(what, value)

        def steps_of_heads(eng, step):
            step(0, True, False)
            with eng.Fori(1, NKV - 1) as kv:
                step(kv, False, False)
            step(NKV - 1, False, True)

        NK = 16
        WQ0, WO0 = 24, 28
        NF_STEPS = 20

        @block.sync
        def _(sp):
            def piece(n, src, slot, rounds):
                wait(sp, piece_lo, n - 3)
                sp.dma_start(stage[:, slot, :], src).then_inc(piece_in[slot], 16)

            def nf_load(col, c):
                wait(sp, nf_step, NF_STEPS * c)
                sp.dma_start(nfv[:, :], nf_d[:, bass.ds(col, CH)]).then_inc(nf_in, 16)

            def nf_store(dst, c):
                wait(sp, nf_step, NF_STEPS * c + NF_STEPS)
                sp.dma_start(dst, nfa[:, :]).then_inc(nf_out, 16)

            def k_store(u):
                wait(sp, roped, u + 1)
                c, half, kvl = u // 8, u % 8 // 4, u % 4
                sp.dma_start(ks_d[4 * c + kvl, half], qT[:, u % 8 // 4, u % 4, :]).then_inc(k_out[u % 8], 16)

            for n in range(4):
                piece(n, ctx_t[n], n, 0)
            sp.dma_start(tab[:, :, :], table_d).then_inc(tab_in, 16)
            sp.dma_start(mt8[:, :], mask_t).then_inc(mask_in, 16)
            for n in range(4, 8):
                piece(n, wk_d[n - 4], n % 4, 0)
            sp.dma_start(y[:, :, :], x_d.rearrange("b s d -> s b d")).then_inc(x_in, 16)
            nf_load(8 * CH, 0)
            for n in range(8, 20):
                piece(n, ctx_t[n - 4] if n < 12 else wk_d[n - 8] if n < 16 else wv_d[n - 16], n % 4, 0)
            for u in range(8):
                k_store(u)
            for n in range(20, 24):
                piece(n, wv_d[n - 16], n % 4, 0)
            for u in range(8, 16):
                k_store(u)
            nf_store(dq3[:, 0:CH], 0)
            nf_load(9 * CH, 1)
            for n in range(24, 28):
                piece(n, wq_d[n - WQ0], n % 4, 0)
            for v in range(16):
                c, b = v // B, v % B
                wait(sp, v_copied, v + 1)
                sp.dma_start(vs_d[4 * c:4 * c + 4, b // 4, :, b % 4, :].rearrange("k t d -> t k d"),
                             vst[:, v % 4, :].rearrange("t (k d) -> t k d", k=4)).then_inc(v_out[v % 4], 16)
            for n in range(28, 32):
                piece(n, wo_d[n - WO0], n % 4, 0)
            nf_store(dq3[:, CH:2 * CH], 1)
            for i in range(8):
                wait(sp, k_out[i], 32)
            for i in range(4):
                wait(sp, v_out[i], 64)
            wait(sp, consts, 2)
            sp.dma_start(kcur[:, 0, :], ks_d[0, 0]).then_inc(k_in[0], 16)
            sp.dma_start(vcur[:, 0:4, 0:DH], vs_d[0, 0]).then_inc(v_in[0], 16)

            def head(kv, first, last):
                wait(sp, logits_done, 8 * kv)
                sp.dma_start(kcur[:, 1, :], ks_d[kv, 1]).then_inc(k_in[1], 16)
                wait(sp, av_done, 8 * kv)
                sp.dma_start(vcur[:, 4:8, 0:DH], vs_d[kv, 1]).then_inc(v_in[1], 16)
                nf_load(kv * CH, kv + 2)
                if not last:
                    for g in range(G):
                        piece(8 * kv + 32 + g, wq_d[kv * 4 + 4 + g], g, 0)
                    wait(sp, logits_done, 8 * kv + 4)
                    sp.dma_start(kcur[:, 0, :], ks_d[kv + 1, 0]).then_inc(k_in[0], 16)
                    wait(sp, av_done, 8 * kv + 4)
                    sp.dma_start(vcur[:, 0:4, 0:DH], vs_d[kv + 1, 0]).then_inc(v_in[0], 16)
                    for g in range(G):
                        piece(8 * kv + 36 + g, wo_d[kv * 4 + 4 + g], g, 0)
                nf_store(dq12[:, bass.ds(kv * CH, CH)], kv + 2)

            steps_of_heads(sp, head)

            nf_load(10 * CH, 10)
            wait(sp, nf_out, 16 * 10)
            for n in range(2 * HT):
                if n == 16:
                    nf_store(dq3[:, 2 * CH:3 * CH], 10)
                    nf_load(11 * CH, 11)
                wait(sp, wt_done, n - 3)
                if n < 4:
                    wait(sp, piece_lo, 88)
                sp.dma_start(stage[:, n % 4, :], dq12[:, (n % 2) * NFW + (n // 2) * D:(n % 2) * NFW + (n // 2 + 1) * D])\
                    .then_inc(piece_in[n % 4], 16)
            nf_store(dq3[:, 3 * CH:4 * CH], 11)
            wait(sp, nf_out, 16 * 12)
            w3v = dq3[:, 0:4 * HID].rearrange("p (i h) -> p i h", i=4)
            for n in range(HT):
                m = 2 * HT + n
                cols = 128 if n < HT - 1 else HLAST
                wait(sp, wt_done, m - 3)
                sp.dma_start(stage[:, m % 4, :].rearrange("p (i h) -> p i h", i=4)[:, :, 0:cols],
                             w3v[:, :, n * 128:n * 128 + cols]).then_inc(piece_in[m % 4], 16)
            for b in range(B):
                wait(sp, final_done, b + 1)
                sp.dma_start(out_d[b], y[:, b, :]).then_inc(stored, 16)
            wait(sp, stored, 16 * B)

        @block.tensor
        def _(pe):
            def three(out, pairs):
                n = len(pairs)
                for i, (wh, wl, mh, ml) in enumerate(pairs):
                    nc.tensor.matmul(out, wh, mh, start=i == 0, stop=False)
                    nc.tensor.matmul(out, wh, ml, start=False, stop=False)
                    last = nc.tensor.matmul(out, wl, mh, start=False, stop=i == n - 1)
                return last

            def transpose4(out, src, p=128):
                for i in range(4):
                    last = nc.tensor.transpose(out[0:p, i * 128:(i + 1) * 128], src(i), tab[:, 2, :])
                return last

            def q_unit(ru, g, half):
                wait(pe, cos_done, ru - 1)
                three(prj[g % 2][:, :], [(wqh[:, g, k, :], wql[:, g, k, :],
                                          xh[:, k, half * 512:(half + 1) * 512],
                                          xl[:, k, half * 512:(half + 1) * 512]) for k in range(KT)])\
                    .then_inc(proj_done, 1)

            def out_mm(slot, heads):
                for g in heads:
                    o = prj2[slot % 2][:, :]
                    ah, al = ath[:, slot, g * 128:(g + 1) * 128], atl[:, slot, g * 128:(g + 1) * 128]
                    nc.tensor.matmul(o, ah, woh[:, g, :], start=g == 0, stop=False)
                    nc.tensor.matmul(o, ah, wol[:, g, :], start=False, stop=False)
                    last = nc.tensor.matmul(o, al, woh[:, g, :], start=False, stop=g == G - 1)
                return last

            pe.wait_ge(masks, 1)
            pe.wait_ge(consts, 1)
            nc.tensor.matmul(trp[:, 0:S], ones[:, :], maskf[:, :], start=True, stop=True).then_inc(mask_count, 1)
            for u in range(NK):
                c, half, kvl = u // 8, u % 8 // 4, u % 4
                if u == 0:
                    pe.wait_ge(piece_lo, 8)
                if u == 4:
                    pe.wait_ge(piece_lo, 12)
                if u == 8:
                    pe.wait_ge(piece_lo, 16)
                wait(pe, cos_done, u - 1)
                cs = slice(half * 512, (half + 1) * 512)
                three(prj[u % 2][:, :], [(wch[c][:, k, kvl * 128:(kvl + 1) * 128], wcl[c][:, k, kvl * 128:(kvl + 1) * 128],
                                          cth[:, k, cs], ctl[:, k, cs]) for k in range(KT)]).then_inc(proj_done, 1)
                if u >= 4 and u < 12:
                    i = u - 4
                    pe.wait_ge(xn_done, i + 1)
                    wait(pe, xt_lo, i)
                    if i == 0:
                        pe.wait_ge(masks, 2)
                        pe.wait_ge(tab_in, 16)
                    transpose4(trp, lambda k: nrm[:, i % 2, k * 128:(k + 1) * 128]).then_inc(xt_done, 1)
            for v in range(16):
                c, b = v // B, v % B
                if v % B == 0:
                    pe.wait_ge(piece_lo, 20 + 4 * c)
                wait(pe, v_copied, v - 1)
                bs = slice(b * 128, (b + 1) * 128)
                three(prj2[v % 2][:, :], [(cth[:, k, bs], ctl[:, k, bs], wch[c][:, k, :], wcl[c][:, k, :])
                                          for k in range(KT)]).then_inc(vproj_done, 1)
            pe.wait_ge(xt_lo, 8)
            for g in range(G):
                pe.wait_ge(piece_lo, WQ0 + g + 1)
                q_unit(NK + g, g, 0)

            def head(kv, first, last):
                for b in range(B):
                    j, h, s = 8 * kv + b, b // 4, b % 4
                    prev = not (first and b == 0)
                    if s == 0:
                        pe.wait_ge(roped, NK + 8 * kv + 4 * h + 4)
                        pe.wait_ge(k_in[h], 16 * kv + 16)
                    wait(pe, tanh_done, j)
                    nc.tensor.matmul(lgp[:, :], kcur[:, h, s * 128:(s + 1) * 128],
                                     qT[:, h, :, s * 128:(s + 1) * 128], start=True, stop=True)\
                        .then_inc(logits_done, 1)
                    if prev:
                        pe.wait_ge(an_done, j)
                        wait(pe, at_lo, j - 1)
                        transpose4(trp, lambda g: nrm[:, (b + 1) % 2, g * 128:(g + 1) * 128]).then_inc(at_done, 1)
                    if s in (0, 3):
                        for n in range(2):
                            slot = 2 + n if s == 0 else n
                            unit = j - 2 + n if s == 0 else j - 3 + n
                            if s == 0 and not prev:
                                continue
                            if s == 3 and h == 0 and n == 0:
                                pe.wait_ge(piece_lo, 8 * kv + WO0 + 4)
                            pe.wait_ge(at_lo, unit + 1)
                            wait(pe, y_done, unit - 1)
                            if n == 0:
                                out_mm(slot, range(G)).then_inc(out_done, 1)
                            else:
                                out_mm(slot, range(3))
                        if s == 0 and not prev:
                            pending = None
                        else:
                            pending = slot
                    else:
                        pending = None
                        if not (last and h == 1):
                            for n in range(2):
                                g = 2 * (s - 1) + n
                                if h == 1:
                                    pe.wait_ge(piece_lo, 8 * kv + 33 + g)
                                q_unit(8 * kv + NK + 4 * h + 4 + g, g, 1 - h)
                    pe.wait_ge(weights_done, j + 1)
                    if s == 0:
                        pe.wait_ge(v_in[h], 16 * kv + 16)
                    wait(pe, an_done, j)
                    for g in range(G):
                        av = nc.tensor.matmul(avp[:, g // 2, (g % 2) * (DH + 1):(g % 2 + 1) * (DH + 1)],
                                              eb[:, b % 2, g * 128:(g + 1) * 128], vcur[:, b, :],
                                              start=True, stop=True)
                    av.then_inc(av_done, 1)
                    if pending is not None:
                        out_mm(pending, range(3, G)).then_inc(out_done, 1)

            steps_of_heads(pe, head)
            n_steps = NKV * B
            pe.wait_ge(an_done, n_steps)
            pe.wait_ge(at_lo, n_steps - 1)
            transpose4(trp, lambda g: nrm[:, 1, g * 128:(g + 1) * 128]).then_inc(at_done, 1)
            for unit in (n_steps - 2, n_steps - 1):
                pe.wait_ge(at_lo, unit + 1)
                pe.wait_ge(y_done, unit - 1)
                out_mm(unit % 4, range(G)).then_inc(out_done, 1)

            def weight_transposes(n):
                pe.wait_ge(piece_in[n % 4], 16 * (22 + n // 4 + 1))
                wait(pe, wt_lo, n - 1)
                if n == 1:
                    pe.wait_ge(tanh_done, n_steps)
                transpose4(trg[n % 2], lambda k: stage[:, n % 4, k * 128:(k + 1) * 128]).then_inc(wt_done, 1)

            pe.wait_ge(at_lo, n_steps)
            weight_transposes(0)
            weight_transposes(1)
            for b in range(B):
                pe.wait_ge(xn_done, 8 + b + 1)
                wait(pe, xt_lo, 8 + b - 1)
                if b == 0:
                    pe.wait_ge(an_done, n_steps)
                transpose4(avp[:, b % 2, :], lambda k: nrm[:, b % 2, k * 128:(k + 1) * 128]).then_inc(xt_done, 1)
            for t in range(HT):
                if t < HT - 1:
                    weight_transposes(2 * t + 2)
                    weight_transposes(2 * t + 3)
                pe.wait_ge(wt_lo, 2 * t + 2)
                for half in range(2):
                    n = 2 * t + half
                    if n < 2:
                        pe.wait_ge(xt_lo, 8 + 4 * (half + 1))
                        pe.wait_ge(y_done, n_steps)
                    wait(pe, h_done, n - 1)
                    cs = slice(half * 512, (half + 1) * 512)
                    for w, o in ((0, prj), (1, prj2)):
                        last = three(o[n % 2][:, :], [(wgh[:, t % 2, w, k, :], wgl[:, t % 2, w, k, :],
                                                       xh[:, k, cs], xl[:, k, cs]) for k in range(KT)])
                    last.then_inc(gate_done, 1)

            def w3_transposes(n):
                m = 2 * HT + n
                p = 128 if n < HT - 1 else HLAST
                pe.wait_ge(piece_in[m % 4], 16 * (22 + m // 4 + 1))
                wait(pe, wt_lo, m - 1)
                transpose4(trg[m % 2], lambda i: stage[:, m % 4, i * 128:i * 128 + p], p).then_inc(wt_done, 1)

            def down(b, n, o):
                p = 128 if n < HT - 1 else HLAST
                ah, al = hh[0:p, n, b * 128:(b + 1) * 128], hl[0:p, n, b * 128:(b + 1) * 128]
                nc.tensor.matmul(o, ah, w3h[0:p, n, :], start=n == 0, stop=False)
                nc.tensor.matmul(o, ah, w3l[0:p, n, :], start=False, stop=False)
                return nc.tensor.matmul(o, al, w3h[0:p, n, :], start=False, stop=n == HT - 1)

            outs = [prj[0], prj[1], prj2[0], prj2[1]]
            w3_transposes(0)
            w3_transposes(1)
            for n in range(HT):
                pe.wait_ge(wt_lo, 2 * HT + n + 1)
                if n == 0:
                    pe.wait_ge(h_lo, 2 * HT)
                for b in range(4):
                    last = down(b, n, outs[b][:, :])
                    if n == HT - 1:
                        last.then_inc(down_done, 1)
                if n < HT - 2:
                    w3_transposes(n + 2)
            for b in range(4, B):
                pe.wait_ge(final_done, b - 3)
                for n in range(HT):
                    last = down(b, n, outs[b - 4][:, :])
                last.then_inc(down_done, 1)

        @block.scalar
        def _(act):
            def nf_above_bound(c, i):
                wait(act, nf_step, NF_STEPS * c + (4 if i < 2 else 3 + i))
                nc.scalar.activation(nfp[:, i % 2, :], nfv[:, :], ACT.Sign, bias=bnd[:, i:i + 1])\
                    .then_inc(nf_above, 1)

            def swap(ru, slot):
                act.wait_ge(proj_done, ru + 1)
                wait(act, roped, ru - 1)
                nc.scalar.activation(sw[0:64, slot, :], prj[slot][64:128, :], ACT.Copy)
                nc.scalar.activation(sw[64:128, slot, :], prj[slot][0:64, :], ACT.Copy).then_inc(swapped, 1)

            act.wait_ge(ln_stat, 1)
            nc.scalar.activation(std[:, :], veps[:, :], ACT.Sqrt).then_inc(ln_std, 1)
            for u in range(NK):
                swap(u, u % 2)
                if u >= 4 and u < 12:
                    i = u - 4
                    act.wait_ge(xt_done, i + 1)
                    nc.scalar.activation(xh[:, :, i * 128:(i + 1) * 128],
                                         trp[:, :].rearrange("p (k t) -> p k t", k=KT), ACT.Copy).then_inc(xt_hi, 1)
                if u >= 1:
                    if u == 1:
                        act.wait_ge(consts, 3)
                    nf_above_bound(0, u - 1)
            for v in range(16):
                act.wait_ge(vproj_done, v + 1)
                wait(act, v_out[v % 4], 16 * (v // 4))
                nc.scalar.activation(vst[:, v % 4, :], prj2[v % 2][:, :], ACT.Copy).then_inc(v_copied, 1)
                if v >= 1:
                    nf_above_bound(1, v - 1)
            for g in range(G):
                swap(NK + g, g % 2)

            def head(kv, first, last):
                for b in range(B):
                    j, h, s = 8 * kv + b, b // 4, b % 4
                    act.wait_ge(logits_done, j + 1)
                    wait(act, av_done, j - 1)
                    nc.scalar.activation(eb[:, b % 2, :], lgp[:, :], ACT.Tanh, scale=MULT / CAP).then_inc(tanh_done, 1)
                    act.wait_ge(tanh_done, j + 1)
                    nc.scalar.activation(eb[:, b % 2, :], eb[:, b % 2, :], ACT.Exp, scale=CAP).then_inc(exp_done, 1)
                    if not (first and b == 0):
                        act.wait_ge(at_done, j)
                        wait(act, out_done, j - 4)
                        nc.scalar.activation(ath[:, (b + 3) % 4, :], trp[:, :], ACT.Copy).then_inc(at_hi, 1)
                    if b > 0:
                        nf_above_bound(kv + 2, 2 * b - 1)
                    if s in (1, 2) and not (last and h == 1):
                        swap(8 * kv + NK + 4 * h + 4 + 2 * (s - 1), 0)
                    if b == 0:
                        nf_above_bound(kv + 2, 0)
                    if b > 0:
                        nf_above_bound(kv + 2, 2 * b)
                    if s in (1, 2) and not (last and h == 1):
                        swap(8 * kv + NK + 4 * h + 5 + 2 * (s - 1), 1)

            steps_of_heads(act, head)
            n_steps = NKV * B
            act.wait_ge(at_done, n_steps)
            act.wait_ge(out_done, n_steps - 4)
            nc.scalar.activation(ath[:, 3, :], trp[:, :], ACT.Copy).then_inc(at_hi, 1)

            act.wait_ge(ln_stat, 2)
            nc.scalar.activation(std[:, :], veps[:, :], ACT.Sqrt).then_inc(ln_std, 1)

            def weight_hi(n):
                act.wait_ge(wt_done, n + 1)
                wait(act, gate_done, 2 * (n // 2 - 1))
                if n == 0:
                    act.wait_ge(out_done, n_steps)
                nc.scalar.activation(wgh[:, n // 2 % 2, n % 2, :, :],
                                     trg[n % 2][:, :].rearrange("p (k h) -> p k h", k=KT), ACT.Copy).then_inc(wt_hi, 1)

            weight_hi(0)
            weight_hi(1)
            for b in range(B):
                act.wait_ge(xt_done, 8 + b + 1)
                nc.scalar.activation(xh[:, :, b * 128:(b + 1) * 128],
                                     avp[:, b % 2, :].rearrange("p (k t) -> p k t", k=KT), ACT.Copy).then_inc(xt_hi, 1)
            for t in range(HT):
                if t < HT - 1:
                    weight_hi(2 * t + 2)
                    weight_hi(2 * t + 3)
                for half in range(2):
                    n = 2 * t + half
                    for i in range(15 * n // 11, 15 * (n + 1) // 11):
                        nf_above_bound(10 + i // 15, i % 15)
                    act.wait_ge(gate_done, n + 1)
                    wait(act, h_done, n - 1)
                    nc.scalar.activation(sg[:, n % 2, :], prj[n % 2][:, :], ACT.Silu).then_inc(silu_done, 1)
            for n in range(HT):
                m = 2 * HT + n
                p = 128 if n < HT - 1 else HLAST
                act.wait_ge(wt_done, m + 1)
                if n == 0:
                    act.wait_ge(gate_done, 2 * HT)
                nc.scalar.activation(w3h[0:p, n, :].rearrange("h (a r q) -> h a q r", a=2, q=2),
                                     trg[m % 2][0:p, :].rearrange("h (a q r) -> h a q r", a=2, q=2), ACT.Copy)\
                    .then_inc(wt_hi, 1)

        @block.vector
        def _(dve):
            def as_f32(ap):
                return ap.bitcast(f32)

            def batches(table):
                return table.rearrange("p (o t) -> p o t", o=1).to_broadcast([128, 4, S])

            def blocks(ap):
                return ap.rearrange("p (b e) -> p b e", e=BLK)

            def spread(ap):
                return ap.rearrange("p (b o) -> p b o", o=1).to_broadcast([128, CH // BLK, BLK])

            def nf(c, i):
                if i == 0:
                    dve.wait_ge(nf_in, 16 * c + 16)
                if i > 0 or not isinstance(c, int) or c > 0:
                    dve.wait_ge(nf_step, NF_STEPS * c + i)
                if i == 0:
                    op = nc.vector.tensor_reduce(nfm[:, :], blocks(nfv[:, :]), axis=AX.X, op=ALU.max,
                                                 apply_absolute_value=True)
                elif i == 1:
                    op = nc.vector.scalar_tensor_tensor(nfg[:, :], nfm[:, :], 0.0, nfm[:, :], ALU.is_equal, ALU.add)
                elif i == 2:
                    op = nc.vector.reciprocal(nfr[:, :], nfg[:, :])
                elif i == 3:
                    op = nc.vector.tensor_tensor(blocks(nfv[:, :]), blocks(nfv[:, :]), spread(nfr[:, :]), ALU.mult)
                elif i < 19:
                    b = i - 4
                    dve.wait_ge(nf_above, 15 * c + b + 1)
                    if b == 0:
                        if not isinstance(c, int) or c > 0:
                            dve.wait_ge(nf_out, 16 * c)
                        op = nc.vector.tensor_scalar(nfa[:, :], nfp[:, 0, :], STEPS[0], NF4_CODE[0], ALU.mult, ALU.add)
                    else:
                        op = nc.vector.scalar_tensor_tensor(nfa[:, :], nfp[:, b % 2, :], STEPS[b], nfa[:, :],
                                                            ALU.mult, ALU.add)
                else:
                    op = nc.vector.tensor_tensor(blocks(nfa[:, :]), blocks(nfa[:, :]), spread(nfm[:, :]), ALU.mult)
                op.then_inc(nf_step, 1)

            def piece(n, slot, rounds, hi):
                dve.wait_ge(piece_in[slot], 16 * rounds)
                nc.vector.tensor_copy(hi, stage[:, slot, :]).then_inc(piece_hi, 1)

            def cos_part(ru, slot, dst, cos):
                dve.wait_ge(swapped, ru + 1)
                nc.vector.tensor_tensor(dst.rearrange("p (b t) -> p b t", b=4),
                                        prj[slot][:, :].rearrange("p (b t) -> p b t", b=4), batches(cos), ALU.mult)\
                    .then_inc(cos_done, 1)

            nc.vector.memset(ones[:, :], 1.0).then_inc(consts, 1)
            nc.vector.memset(vcur[:, :, :], 1.0).then_inc(consts, 1)
            for i in range(15):
                last = nc.vector.memset(bnd[:, i:i + 1], -BOUNDS[i])
            last.then_inc(consts, 1)
            dve.wait_ge(mask_in, 16)
            nc.vector.tensor_copy(maskf[:, :], mt8[:, :]).then_inc(masks, 1)

            def static_hi(n):
                k, c = n % 4, n // 4
                hi = {0: lambda: cth[:, k, 0:512], 1: lambda: wch[0][:, k, :], 2: lambda: cth[:, k, 512:1024],
                      3: lambda: wch[1][:, k, :], 4: lambda: wch[0][:, k, :], 5: lambda: wch[1][:, k, :],
                      6: lambda: wqh[:, k, :, :].rearrange("p k n -> p (k n)")}[c]()
                if n == 16:
                    dve.wait_ge(proj_done, 8)
                if n == 20:
                    dve.wait_ge(proj_done, 16)
                piece(n, n % 4, n // 4 + 1, hi)

            for n in range(8):
                static_hi(n)
            dve.wait_ge(mask_count, 1)
            dve.wait_ge(tab_in, 16)
            nc.vector.tensor_scalar(nomask[:, :], trp[:, 0:S], 0.5, None, ALU.is_lt).then_inc(mask_step, 1)
            nc.vector.tensor_scalar(keep[:, :], trp[:, 0:S], 0.5, None, ALU.is_gt).then_inc(mask_step, 1)
            dve.wait_ge(mask_step, 2)
            nc.vector.tensor_tensor(maskf[:, :], maskf[:, :], nomask[:, :], ALU.add)
            nc.vector.tensor_tensor(cosq[:, :], tab[:, 0, :], keep[:, :], ALU.mult)
            nc.vector.tensor_tensor(sinq[:, :], tab[:, 1, :], keep[:, :], ALU.mult).then_inc(masks, 1)

            def ln_stats(round):
                for b in range(B):
                    if round == 1:
                        dve.wait_ge(y_done, NKV * B - B + b + 1)
                    last = nc.vector.bn_stats(stat[:, b, :], y[:, b, :])
                last.then_inc(stat_step, 1)
                dve.wait_ge(stat_step, 3 * round + 1)
                for b in range(B):
                    last = nc.vector.bn_aggr(mv[:, b, :], stat[:, b, :])
                last.then_inc(stat_step, 1)
                dve.wait_ge(stat_step, 3 * round + 2)
                nc.vector.tensor_scalar(veps[:, :], mv[:, :, 1], EPS, None, ALU.add).then_inc(ln_stat, 1)
                dve.wait_ge(ln_std, round + 1)
                nc.vector.reciprocal(rstd[:, :], std[:, :]).then_inc(stat_step, 1)
                dve.wait_ge(stat_step, 3 * round + 3)

            def normalise(b):
                nc.vector.tensor_scalar(nrm[:, b % 2, :], y[:, b, :], mv[:, b, 0:1], rstd[:, b:b + 1],
                                        ALU.subtract, ALU.mult).then_inc(xn_done, 1)

            def token_lo(b, round, src):
                dve.wait_ge(xt_hi, 8 * round + b + 1)
                ts = slice(b * 128, (b + 1) * 128)
                nc.vector.tensor_tensor(xl[:, :, ts], src.rearrange("p (k t) -> p k t", k=KT),
                                        as_f32(xh[:, :, ts]), ALU.subtract).then_inc(xt_lo, 1)

            for n in range(8, 12):
                static_hi(n)
            dve.wait_ge(x_in, 16)
            ln_stats(0)
            for n in range(12, 16):
                static_hi(n)
            normalise(0)
            normalise(1)
            for u in range(NK):
                if u >= 8:
                    dve.wait_ge(k_out[u - 8], 16)
                cos_part(u, u % 2, qT[:, u % 8 // 4, u % 4, :], tab[:, 0, :])
                if u >= 4 and u < 12:
                    i = u - 4
                    token_lo(i, 0, trp[:, :])
                    if i + 2 < B:
                        dve.wait_ge(xt_done, i + 1)
                        normalise(i + 2)
                if u >= 8 and u < 12:
                    static_hi(u + 8)
                if u == 0:
                    for i in range(4):
                        nf(0, i)
                else:
                    nf(0, 3 + u)
            nf(0, 19)
            for n in range(20, 28):
                static_hi(n)
            for i in range(NF_STEPS):
                nf(1, i)
            for g in range(G):
                if g == 0:
                    for i in range(4):
                        dve.wait_ge(k_out[i], 32)
                cos_part(NK + g, g % 2, qT[:, 0, g, :], cosq[:, :])

            def head(kv, first, last):
                for b in range(B):
                    j, h, s = 8 * kv + b, b // 4, b % 4
                    prev = not (first and b == 0)
                    if prev:
                        dve.wait_ge(at_hi, j)
                        nc.vector.tensor_tensor(atl[:, (b + 3) % 4, :], trp[:, :], as_f32(ath[:, (b + 3) % 4, :]),
                                                ALU.subtract).then_inc(at_lo, 1)
                    for n in range(2):
                        if b in (1, 2):
                            g = 2 * (b - 1) + n
                            if g == 0:
                                wait(dve, out_done, 8 * kv)
                                if first:
                                    dve.wait_ge(vproj_done, 16)
                            piece(0, g, 2 * kv + 8, woh[:, g, :])
                        if b in (3, 4) and not last:
                            g = 2 * (b - 3) + n
                            if g == 0:
                                dve.wait_ge(proj_done, 8 * kv + NK + 8)
                            piece(0, g, 2 * kv + 9, wqh[:, g, :, :].rearrange("p k n -> p (k n)"))
                    if b == 0:
                        for i in range(4):
                            nf(kv + 2, i)
                    else:
                        nf(kv + 2, 2 * b + 3)

                    def project(n):
                        if s in (0, 3):
                            if s == 0 and not prev:
                                return
                            unit = j - 2 + n if s == 0 else j - 3 + n
                            batch = (b - 2 + n) % 8 if s == 0 else b - 3 + n
                            dve.wait_ge(out_done, unit + 1)
                            nc.vector.tensor_tensor(y[:, batch, :], prj2[n][:, :], y[:, batch, :], ALU.add)\
                                .then_inc(y_done, 1)
                        elif not (last and h == 1):
                            g = 2 * (s - 1) + n
                            cos_part(8 * kv + NK + 4 * h + 4 + g, g % 2, qT[:, 1 - h, g, :], cosq[:, :])

                    project(0)
                    if b == 0:
                        nf(kv + 2, 4)
                    else:
                        nf(kv + 2, 2 * b + 4)
                    dve.wait_ge(av_done, j + 1)
                    nc.vector.reciprocal(rs[:, :].rearrange("p (a c) -> p a c", a=2),
                                         avp[:, :, DH:2 * (DH + 1):DH + 1]).then_inc(recip_done, 1)
                    dve.wait_ge(recip_done, j + 1)
                    nc.vector.tensor_tensor(
                        nrm[:, b % 2, :].rearrange("p (a c d) -> p a c d", a=2, c=2),
                        avp[:, :, 0:2 * (DH + 1)].rearrange("p a (c d) -> p a c d", c=2)[:, :, :, 0:DH],
                        rs[:, :].rearrange("p (a c o) -> p a c o", a=2, c=2).to_broadcast([128, 2, 2, DH]),
                        ALU.mult).then_inc(an_done, 1)
                    project(1)
                nf(kv + 2, 19)

            steps_of_heads(dve, head)
            n_steps = NKV * B
            dve.wait_ge(at_hi, n_steps)
            nc.vector.tensor_tensor(atl[:, 3, :], trp[:, :], as_f32(ath[:, 3, :]), ALU.subtract).then_inc(at_lo, 1)
            for unit in (n_steps - 2, n_steps - 1):
                dve.wait_ge(out_done, unit + 1)
                nc.vector.tensor_tensor(y[:, unit % 8, :], prj2[unit % 2][:, :], y[:, unit % 8, :], ALU.add)\
                    .then_inc(y_done, 1)

            def weight_lo(n):
                dve.wait_ge(wt_hi, n + 1)
                nc.vector.tensor_tensor(wgl[:, n // 2 % 2, n % 2, :, :],
                                        trg[n % 2][:, :].rearrange("p (k h) -> p k h", k=KT),
                                        as_f32(wgh[:, n // 2 % 2, n % 2, :, :]), ALU.subtract).then_inc(wt_lo, 1)

            ln_stats(1)
            normalise(0)
            normalise(1)
            weight_lo(0)
            weight_lo(1)
            for b in range(B):
                token_lo(b, 1, avp[:, b % 2, :])
                if b + 2 < B:
                    dve.wait_ge(xt_done, 8 + b + 1)
                    normalise(b + 2)
            for t in range(HT):
                if t < HT - 1:
                    weight_lo(2 * t + 2)
                    weight_lo(2 * t + 3)
                for half in range(2):
                    n = 2 * t + half
                    if n == 0 or n == 11:
                        for i in range(4):
                            nf(10 + n // 11, i)
                    dve.wait_ge(silu_done, n + 1)
                    wait(dve, h_lo, n - 1)
                    nc.vector.tensor_tensor(hf[:, n % 2, :], prj2[n % 2][:, :], sg[:, n % 2, :], ALU.mult)\
                        .then_inc(h_done, 1)
                    dve.wait_ge(h_done, n + 1)
                    nc.vector.tensor_copy(hh[:, t, half * 512:(half + 1) * 512], hf[:, n % 2, :]).then_inc(h_hi, 1)
                    for i in range(15 * n // 11, 15 * (n + 1) // 11):
                        nf(10 + i // 15, 4 + i % 15)
                        if i % 15 == 14:
                            nf(10 + i // 15, 19)
            for n in range(HT):
                m = 2 * HT + n
                p = 128 if n < HT - 1 else HLAST
                dve.wait_ge(wt_hi, m + 1)
                nc.vector.tensor_tensor(w3l[0:p, n, :].rearrange("h (a r q) -> h a q r", a=2, q=2),
                                        trg[m % 2][0:p, :].rearrange("h (a q r) -> h a q r", a=2, q=2),
                                        as_f32(w3h[0:p, n, :]).rearrange("h (a r q) -> h a q r", a=2, q=2),
                                        ALU.subtract).then_inc(wt_lo, 1)
            outs = [prj[0], prj[1], prj2[0], prj2[1]]
            for b in range(B):
                dve.wait_ge(down_done, b + 1)
                nc.vector.tensor_tensor(y[:, b, :], outs[b % 4][:, :], y[:, b, :], ALU.add).then_inc(final_done, 1)

        @block.gpsimd
        def _(pool):
            def low(slot, hi, lo, n):
                pool.wait_ge(piece_hi, n + 1)
                nc.gpsimd.tensor_tensor(lo, stage[:, slot, :], hi.bitcast(f32), ALU.subtract).then_inc(piece_lo, 1)

            def flat(ap):
                return ap.rearrange("p k n -> p (k n)")

            def rope(ru, slot, dst, sin):
                pool.wait_ge(swapped, ru + 1)
                part = sw[:, slot, :].rearrange("p (b t) -> p b t", b=4)
                nc.gpsimd.tensor_tensor(part, part, sin.rearrange("p (o t) -> p o t", o=1).to_broadcast([128, 4, S]),
                                        ALU.mult).then_inc(sin_done, 1)
                pool.wait_ge(cos_done, ru + 1)
                pool.wait_ge(sin_done, ru + 1)
                nc.gpsimd.tensor_tensor(dst, dst, sw[:, slot, :], ALU.add).then_inc(roped, 1)

            def static_low(n):
                k, c = n % 4, n // 4
                hi, lo = {0: lambda: (cth[:, k, 0:512], ctl[:, k, 0:512]), 1: lambda: (wch[0][:, k, :], wcl[0][:, k, :]),
                          2: lambda: (cth[:, k, 512:1024], ctl[:, k, 512:1024]),
                          3: lambda: (wch[1][:, k, :], wcl[1][:, k, :]), 4: lambda: (wch[0][:, k, :], wcl[0][:, k, :]),
                          5: lambda: (wch[1][:, k, :], wcl[1][:, k, :]),
                          6: lambda: (flat(wqh[:, k, :, :]), flat(wql[:, k, :, :]))}[c]()
                low(n % 4, hi, lo, n)

            for n in range(16):
                static_low(n)
            pool.wait_ge(tab_in, 16)
            for u in range(NK):
                rope(u, u % 2, qT[:, u % 8 // 4, u % 4, :], tab[:, 1, :])
                if u >= 8 and u < 12:
                    static_low(u + 8)
            for n in range(20, 28):
                static_low(n)
            pool.wait_ge(masks, 2)
            for g in range(G):
                rope(NK + g, g % 2, qT[:, 0, g, :], sinq[:, :])

            def head(kv, first, last):
                for b in range(B):
                    j, h, s = 8 * kv + b, b // 4, b % 4
                    pool.wait_ge(exp_done, j + 1)
                    part = eb[:, b % 2, :].rearrange("p (g t) -> p g t", g=G)
                    nc.gpsimd.tensor_tensor(part, part,
                                            maskf[:, :].rearrange("p (o t) -> p o t", o=1).to_broadcast([128, G, S]),
                                            ALU.mult).then_inc(weights_done, 1)
                    for n in range(2):
                        if b in (1, 2):
                            g = 2 * (b - 1) + n
                            low(g, woh[:, g, :], wol[:, g, :], 8 * kv + WO0 + g)
                        if b in (3, 4) and not last:
                            g = 2 * (b - 3) + n
                            low(g, flat(wqh[:, g, :, :]), flat(wql[:, g, :, :]), 8 * kv + 32 + g)
                    if s in (1, 2) and not (last and h == 1):
                        for n in range(2):
                            g = 2 * (s - 1) + n
                            rope(8 * kv + NK + 4 * h + 4 + g, g % 2, qT[:, 1 - h, g, :], sinq[:, :])

            steps_of_heads(pool, head)
            for n in range(2 * HT):
                t, half = n // 2, n % 2
                cs = slice(half * 512, (half + 1) * 512)
                pool.wait_ge(h_hi, n + 1)
                nc.gpsimd.tensor_tensor(hl[:, t, cs], hf[:, n % 2, :], hh[:, t, cs].bitcast(f32), ALU.subtract)\
                    .then_inc(h_lo, 1)


def kernel(x, ctx_4096, mask_1x1xSxS2_bk0, L0_xattn_Wq, L0_xattn_Wk, L0_xattn_Wv, L0_xattn_Wo,
           L0_ffn_w1, L0_ffn_w2, L0_ffn_w3):
    import concourse.bacc as bacc
    from concourse.bass_utils import run_bass_kernel_spmd

    f = np.ascontiguousarray
    x, ctx_ = np.asarray(x), np.asarray(ctx_4096)
    ct = ctx_.reshape(TOK, D).T.reshape(KT, 128, 2, 512).transpose(2, 0, 1, 3).reshape(8, 128, 512)
    wk = np.asarray(L0_xattn_Wk).reshape(KT, 128, 2, 512).transpose(2, 0, 1, 3).reshape(8, 128, 512)
    wv = np.asarray(L0_xattn_Wv).reshape(KT, 128, 2, 512).transpose(2, 0, 1, 3).reshape(8, 128, 512)
    wq = np.asarray(L0_xattn_Wq).reshape(KT, 128, NQ, 128).transpose(2, 1, 0, 3).reshape(NQ, 128, 512)
    wo = np.asarray(L0_xattn_Wo).reshape(NQ, 128, D)
    w1, w2, w3 = (np.asarray(w) for w in (L0_ffn_w1, L0_ffn_w2, L0_ffn_w3))
    parts = [np.pad(w, ((0, HT * 128 - HID), (0, 0))).reshape(HT, 128, D).transpose(1, 0, 2).reshape(128, NFW)
             for w in (w1, w2)]
    parts.append(np.pad(w3.reshape(2, 128, 2 * HID).transpose(1, 0, 2).reshape(128, 4 * HID),
                        ((0, 0), (0, NFW - 4 * HID))))
    nf = np.concatenate(parts, axis=1)
    mask = f(np.asarray(mask_1x1xSxS2_bk0)[0, 0].T)
    inv = (np.float32(1.0) / np.float32(10000.0) ** (np.arange(0, DH, 2, dtype=np.float32) / np.float32(DH))).astype(np.float32)
    phase = np.tile(np.arange(S, dtype=np.float32)[None, :] * inv[:, None], (2, 1)).astype(np.float32)
    sign = np.where(np.arange(DH) < DH // 2, -1.0, 1.0)[:, None]
    table = np.stack([np.cos(phase), sign * np.sin(phase), np.eye(128)], axis=1).astype(np.float32)

    nc = bacc.Bacc("TRN2", target_bir_lowering=False, num_devices=1)
    arrays = {"x_in": f(x), "ctx_pieces": f(ct), "wk_pieces": f(wk), "wv_pieces": f(wv), "wq_pieces": f(wq),
              "wo_pieces": f(wo), "nf_weights": f(nf), "mask_t": mask, "tables": table}
    args = [nc.dram_tensor(name, a.shape, mybir.dt.from_np(a.dtype), kind="ExternalInput").ap()
            for name, a in arrays.items()]
    out = nc.dram_tensor("out", (B, S, D), mybir.dt.float32, kind="ExternalOutput").ap()
    build(nc, *args, out)
    r = run_bass_kernel_spmd(nc, [arrays], core_ids=[0])
    return r.results[0]["out"]
```

```python
import numpy as np
import concourse.bass as bass
import concourse.mybir as mybir

B, S, D = 8, 128, 512
TOK = B * S
KT = D // 128
NKV, G, DH = 8, 4, 128
NQ = NKV * G
HID = 1376
HT = -(-HID // 128)
HLAST = HID - 128 * (HT - 1)
BLK = 64
NFW = 11 * D
CH = 22 * BLK
NCHUNK = 3 * NFW // CH
MULT, CAP = 0.08838834764831845, 30.0
EPS = 1e-5

NF4_CODE = [-1.0, -0.6961928009986877, -0.5250730514526367, -0.39491748809814453, -0.28444138169288635,
            -0.18477343022823334, -0.09105003625154495, 0.0, 0.07958029955625534, 0.16093020141124725,
            0.24611230194568634, 0.33791524171829224, 0.44070982933044434, 0.5626170039176941,
            0.7229568362236023, 1.0]


def nf4_constants():
    code = np.array(NF4_CODE, np.float32)
    bounds = (code[:-1] + code[1:]) * np.float32(0.5)
    steps = []
    for i in range(15):
        d = np.float32(code[i + 1] - code[i])
        for c in (d, np.nextafter(d, np.float32(9)), np.nextafter(d, np.float32(-9))):
            if np.float32(code[i] + c) == code[i + 1]:
                steps.append(float(c))
                break
    assert len(steps) == 15
    return [float(b) for b in bounds], steps


def build(nc, x_d, ctx_t, wk_d, wv_d, wq_d, wo_d, nf_first, nf_rest, mask_t, table_d, out_d):
    from contextlib import ExitStack
    f32, f32r, u8 = mybir.dt.float32, mybir.dt.float32r, mybir.dt.uint8
    ALU, ACT, AX = mybir.AluOpType, mybir.ActivationFunctionType, mybir.AxisListType
    BOUNDS, STEPS = nf4_constants()
    ctx = ExitStack()
    with ctx:
        def sem(name):
            return ctx.enter_context(nc.semaphore(name))

        def sb(name, shape, dt=f32, where=ctx):
            return where.enter_context(nc.sbuf_tensor(name, shape, dt))

        y = sb("y", [128, B, D])
        tab = sb("tab", [128, 3, 128])
        mt8 = sb("mt8", [128, S], u8)
        maskf = sb("maskf", [128, S])
        nomask = sb("nomask", [128, S])
        keep = sb("keep", [128, S])
        cosq = sb("cosq", [128, S])
        sinq = sb("sinq", [128, S])
        ones = sb("ones", [128, 128])
        stat = sb("stat", [128, B, 6])
        bnd = sb("bnd", [128, 15])
        mv = sb("mv", [128, B, 2])
        veps = sb("veps", [128, B])
        half_neg = sb("half_neg", [128, B])
        guess = sb("guess", [128, B])
        corr = sb("corr", [128, B])
        rstd = sb("rstd", [128, B])
        nfv = sb("nfv", [128, CH])
        nfa = sb("nfa", [128, CH])
        nfp = sb("nfp", [128, 2, CH], u8)
        nfm = sb("nfm", [128, CH // BLK])
        nfg = sb("nfg", [128, CH // BLK])
        nfr = sb("nfr", [128, CH // BLK])
        stage = sb("stage", [128, 4, 512])
        nrm = sb("nrm", [128, 2, D])
        rs = sb("rs", [128, 4])

        with ExitStack() as start:
            early = sb("early", [128, 8, 512], f32, start)
        with ExitStack() as down:
            w3h = sb("w3h", [128, HT, D], f32r, down)
        xh = sb("xh", [128, KT, TOK], f32r)
        xl = sb("xl", [128, KT, TOK], f32r)
        with ExitStack() as ffn:
            hh = sb("hh", [128, HT, TOK], f32r, ffn)
            hl = sb("hl", [128, HT, TOK], f32r, ffn)
            with ExitStack() as down:
                w3l = sb("w3l", [128, HT, D], f32r, down)
            sg = sb("sg", [128, 2, 512], f32, ffn)
            hf = sb("hf", [128, 2, 512], f32, ffn)
            wgh = sb("wgh", [128, 2, 2, KT, 128], f32r, ffn)
            wgl = sb("wgl", [128, 2, 2, KT, 128], f32r, ffn)
        kcur = sb("kcur", [128, 2, 512])
        vcur = sb("vcur", [128, B, DH + 1])
        sw = sb("sw", [128, 2, 512])
        eb = sb("eb", [128, 2, 512])
        qT = sb("qT", [128, 2, G, 512])
        wqh = sb("wqh", [128, G, KT, 128], f32r)
        wql = sb("wql", [128, G, KT, 128], f32r)
        with ExitStack() as kv_phase:
            wch0 = sb("wch0", [128, KT, 512], f32r, kv_phase)
            wcl0 = sb("wcl0", [128, KT, 512], f32r, kv_phase)
            wch1 = sb("wch1", [128, KT, 512], f32r, kv_phase)
            wcl1 = sb("wcl1", [128, KT, 512], f32r, kv_phase)
        wch, wcl = [wch0, wch1], [wcl0, wcl1]
        woh = sb("woh", [128, G, D], f32r)
        wol = sb("wol", [128, G, D], f32r)
        ath = sb("ath", [128, 4, 512], f32r)
        atl = sb("atl", [128, 4, 512], f32r)
        cth = sb("cth", [128, KT, TOK], f32r)
        ctl = sb("ctl", [128, KT, TOK], f32r)
        vst = sb("vst", [128, 4, 512])

        ks_d = nc.dram_tensor("ks_scratch", (NKV, 2, 128, 512), f32, kind="Internal").ap()
        vs_d = nc.dram_tensor("vs_scratch", (NKV, 2, 128, B // 2, DH), f32, kind="Internal").ap()
        dq12 = nc.dram_tensor("dq12_scratch", (128, 2 * NFW), f32, kind="Internal").ap()
        dq3 = nc.dram_tensor("dq3_scratch", (128, NFW), f32, kind="Internal").ap()

        bank = [ctx.enter_context(nc.psum_tensor(f"bank{i}", [128, 512], f32)) for i in range(5)]
        avp = ctx.enter_context(nc.psum_tensor("avp", [128, 2, 512], f32))
        trp = ctx.enter_context(nc.psum_tensor("trp", [128, 512], f32))
        prj, prj2, lgp = [bank[0], bank[1]], [bank[2], bank[3]], bank[4]
        trg = [trp, lgp]

        tab_in, mask_in, x_in = sem("tab_in"), sem("mask_in"), sem("x_in")
        piece_in = [sem(f"piece_in{i}") for i in range(4)]
        early_in = [sem(f"early_in{i}") for i in range(8)]
        piece_hi, piece_lo, piece_lo_dve = sem("piece_hi"), sem("piece_lo"), sem("piece_lo_dve")
        k_out = [sem(f"k_out{i}") for i in range(8)]
        v_out = [sem(f"v_out{i}") for i in range(4)]
        k_in = [sem("k_in0"), sem("k_in1")]
        v_in = [sem("v_in0"), sem("v_in1")]
        nf_in, nf_step, nf_above, nf_out = sem("nf_in"), sem("nf_step"), sem("nf_above"), sem("nf_out")
        consts, masks, mask_count = sem("consts"), sem("masks"), sem("mask_count")
        ln_var, ln_guess, ln_step = sem("ln_var"), sem("ln_guess"), sem("ln_step")
        xn_done, xt_done, xt_hi, xt_lo = sem("xn_done"), sem("xt_done"), sem("xt_hi"), sem("xt_lo")
        proj_done, swapped, cos_done, sin_done, roped = (sem("proj_done"), sem("swapped"), sem("cos_done"),
                                                         sem("sin_done"), sem("roped"))
        vproj_done, v_copied = sem("vproj_done"), sem("v_copied")
        logits_done, tanh_done, exp_done, weights_done = (sem("logits_done"), sem("tanh_done"), sem("exp_done"),
                                                          sem("weights_done"))
        av_done, recip_done, an_done = sem("av_done"), sem("recip_done"), sem("an_done")
        at_done, at_hi, at_lo = sem("at_done"), sem("at_hi"), sem("at_lo")
        out_done, y_done = sem("out_done"), sem("y_done")
        wt_done, wt_hi, wt_lo = sem("wt_done"), sem("wt_hi"), sem("wt_lo")
        gate_done, silu_done, h_done, h_hi, h_lo = (sem("gate_done"), sem("silu_done"), sem("h_done"), sem("h_hi"),
                                                    sem("h_lo"))
        mask_step = sem("mask_step")
        down_done, final_done, stored = sem("down_done"), sem("final_done"), sem("stored")
        block = ctx.enter_context(nc.Block())

        def wait(eng, what, value):
            if not isinstance(value, int) or value > 0:
                eng.wait_ge(what, value)

        def steps_of_heads(eng, step):
            step(0, True, False)
            with eng.Fori(1, NKV - 1) as kv:
                step(kv, False, False)
            step(NKV - 1, False, True)

        NK = 16
        WQ0, WO0 = 24, 28
        NF_STEPS = 20

        def split(eng, n):
            if isinstance(n, int) and n <= WO0:
                wait(eng, piece_lo, (n + 1) // 2)
                wait(eng, piece_lo_dve, n // 2)
            else:
                eng.wait_ge(piece_lo, n - WO0 // 2)

        def source(n):
            if 4 <= n < 12:
                return early[:, n - 4, :], early_in[n - 4], 16
            return stage[:, n % 4, :], piece_in[n % 4], 16 * (1 if n < 4 else n // 4 - 1)

        def parts(n):
            k, c = n % 4, n // 4
            if c in (0, 2):
                return cth[:, k, c * 256:c * 256 + 512], ctl[:, k, c * 256:c * 256 + 512]
            if c < 6:
                i = {1: 0, 3: 1, 4: 0, 5: 1}[c]
                return wch[i][:, k, :], wcl[i][:, k, :]
            return wqh[:, k, :, :].rearrange("p k n -> p (k n)"), wql[:, k, :, :].rearrange("p k n -> p (k n)")

        STAGED = 20
        UNITS = [(0, 0), (1, 0), (0, 1), (1, 1)] + [(t, half) for t in range(2, HT) for half in range(2)]

        def units_of(t):
            return UNITS.index((t, 1)) + 1

        def nf_keys(u):
            return range(9 * (u - 5) // 11, 9 * (u - 4) // 11) if u >= 5 else range(0)

        def nf_values(v):
            if v < 4:
                return 0, range(9 + 6 * v // 4, 9 + 6 * (v + 1) // 4)
            return 1, range(15 * (v - 7) // 9, 15 * (v - 6) // 9) if v >= 7 else range(0)

        def first_query(v):
            return {8: 0, 10: 1, 12: 2, 14: 3}.get(v)

        def nf_ffn(n):
            chunk, m = (10, n - 2) if n < 10 else (11, n - 11)
            return chunk, range(15 * m // 8, 15 * (m + 1) // 8) if 0 <= m < 8 else []

        def nf_head(b):
            return {0: [], 7: [12, 13, 14]}.get(b, [2 * b - 2, 2 * b - 1])

        def wt_bank(n):
            return prj2[n % 2] if n < 2 else trg[n % 2]

        def xt_bank(b):
            return prj[b % 2][:, :] if b < 4 else avp[:, b % 2, :]

        @block.sync
        def _(sp):
            def piece(n, src, slot):
                split(sp, n - 3)
                sp.dma_start(stage[:, slot, :], src).then_inc(piece_in[slot], 16)

            def first_piece(n):
                table, back = [(ctx_t, 0), (wk_d, 4), (ctx_t, 4), (wk_d, 8), (wv_d, 16), (wv_d, 16), (wq_d, WQ0)][n // 4]
                if n >= 12:
                    split(sp, n - 3 if n >= 16 else n - 11)
                dst, arrived, _ = source(n)
                sp.dma_start(dst, table[n - back]).then_inc(arrived, 16)

            def nf_load(src, c):
                wait(sp, nf_above, 15 * c)
                sp.dma_start(nfv[:, :], src).then_inc(nf_in, 16)

            def nf_store(dst, c):
                wait(sp, nf_step, NF_STEPS * c + NF_STEPS)
                sp.dma_start(dst, nfa[:, :]).then_inc(nf_out, 16)

            def k_store(u):
                wait(sp, roped, u + 1)
                c, half, kvl = u // 8, u % 8 // 4, u % 4
                sp.dma_start(ks_d[4 * c + kvl, half], qT[:, u % 8 // 4, u % 4, :]).then_inc(k_out[u % 8], 16)

            for n in range(12):
                first_piece(n)
            sp.dma_start(mt8[:, :], mask_t).then_inc(mask_in, 16)
            sp.dma_start(tab[:, :, :], table_d).then_inc(tab_in, 16)
            for n in range(12, 16):
                first_piece(n)
            sp.dma_start(y[:, :, :], x_d.rearrange("b s d -> s b d")).then_inc(x_in, 16)
            nf_load(nf_first[:, 0:CH], 0)
            for n in range(16, 20):
                first_piece(n)
            for u in range(8):
                k_store(u)
            for n in range(20, 24):
                first_piece(n)
            for u in range(8, 16):
                k_store(u)
            for n in range(24, 28):
                first_piece(n)
            for v in range(16):
                if v == 4:
                    nf_load(nf_first[:, CH:2 * CH], 1)
                if v == 5:
                    nf_store(dq3[:, 0:CH], 0)
                    for n in range(28, 32):
                        piece(n, wo_d[n - WO0], n % 4)
                if v == 8:
                    for i in range(8):
                        wait(sp, k_out[i], 32)
                    for i in range(4):
                        wait(sp, v_out[i], 16)
                    wait(sp, consts, 2)
                    sp.dma_start(kcur[:, 0, :], ks_d[0, 0]).then_inc(k_in[0], 16)
                    sp.dma_start(vcur[:, 0:4, 0:DH], vs_d[0, 0]).then_inc(v_in[0], 16)
                c, b = v // B, v % B
                wait(sp, v_copied, v + 1)
                sp.dma_start(vs_d[4 * c:4 * c + 4, b // 4, :, b % 4, :].rearrange("k t d -> t k d"),
                             vst[:, v % 4, :].rearrange("t (k d) -> t k d", k=4)).then_inc(v_out[v % 4], 16)
            for i in range(4):
                wait(sp, v_out[i], 64)

            def head(kv, first, last):
                wait(sp, logits_done, 8 * kv)
                sp.dma_start(kcur[:, 1, :], ks_d[kv, 1]).then_inc(k_in[1], 16)
                wait(sp, av_done, 8 * kv)
                sp.dma_start(vcur[:, 4:8, 0:DH], vs_d[kv, 1]).then_inc(v_in[1], 16)
                if not last:
                    for g in range(G):
                        piece(8 * kv + 32 + g, wq_d[kv * 4 + 4 + g], g)
                    wait(sp, logits_done, 8 * kv + 4)
                    sp.dma_start(kcur[:, 0, :], ks_d[kv + 1, 0]).then_inc(k_in[0], 16)
                    wait(sp, av_done, 8 * kv + 4)
                    sp.dma_start(vcur[:, 0:4, 0:DH], vs_d[kv + 1, 0]).then_inc(v_in[0], 16)
                    for g in range(G):
                        piece(8 * kv + 36 + g, wo_d[kv * 4 + 4 + g], g)
                if last:
                    wait(sp, nf_out, 16 * 7)
                    for n in range(4):
                        weights_in(n)
                nf_load(nf_first[:, 3 * CH:4 * CH] if last else nf_rest[:, bass.ds(kv * CH, CH)], kv + 3)
                nf_store(dq12[:, bass.ds(kv * CH, CH)], kv + 2)

            def weights_in(n):
                if n < 4:
                    split(sp, 8 * NKV + 24)
                wait(sp, wt_done, n - 3)
                col = (n % 2) * NFW + (n // 2) * D
                sp.dma_start(stage[:, n % 4, :], dq12[:, col:col + D]).then_inc(piece_in[n % 4], 16)

            nf_load(nf_first[:, 2 * CH:3 * CH], 2)
            nf_store(dq3[:, CH:2 * CH], 1)
            steps_of_heads(sp, head)

            wait(sp, nf_out, 16 * 10)
            for n in range(4, 2 * HT):
                if n == 14:
                    nf_load(nf_first[:, 4 * CH:5 * CH], 11)
                if n == 16:
                    nf_store(dq3[:, 2 * CH:3 * CH], 10)
                weights_in(n)
            nf_store(dq3[:, 3 * CH:4 * CH], 11)
            wait(sp, nf_out, 16 * 12)
            w3v = dq3[:, 0:4 * HID].rearrange("p (i h) -> p i h", i=4)
            for n in range(HT):
                m = 2 * HT + n
                cols = 128 if n < HT - 1 else HLAST
                wait(sp, wt_done, m - 3)
                sp.dma_start(stage[:, m % 4, :].rearrange("p (i h) -> p i h", i=4)[:, :, 0:cols],
                             w3v[:, :, n * 128:n * 128 + cols]).then_inc(piece_in[m % 4], 16)
            for b in range(B):
                wait(sp, final_done, b + 1)
                sp.dma_start(out_d[b], y[:, b, :]).then_inc(stored, 16)
            wait(sp, stored, 16 * B)

        @block.tensor
        def _(pe):
            def three(out, pairs):
                n = len(pairs)
                for i, (wh, wl, mh, ml) in enumerate(pairs):
                    nc.tensor.matmul(out, wh, mh, start=i == 0, stop=False)
                    nc.tensor.matmul(out, wh, ml, start=False, stop=False)
                    last = nc.tensor.matmul(out, wl, mh, start=False, stop=i == n - 1)
                return last

            def transpose4(out, src, p=128):
                for i in range(4):
                    last = nc.tensor.transpose(out[0:p, i * 128:(i + 1) * 128], src(i), tab[:, 2, :])
                return last

            def q_unit(ru, g, half):
                wait(pe, cos_done, ru - 1)
                three(prj[g % 2][:, :], [(wqh[:, g, k, :], wql[:, g, k, :],
                                          xh[:, k, half * 512:(half + 1) * 512],
                                          xl[:, k, half * 512:(half + 1) * 512]) for k in range(KT)])\
                    .then_inc(proj_done, 1)

            def out_mm(slot, heads):
                for g in heads:
                    o = prj2[slot % 2][:, :]
                    ah, al = ath[:, slot, g * 128:(g + 1) * 128], atl[:, slot, g * 128:(g + 1) * 128]
                    nc.tensor.matmul(o, ah, woh[:, g, :], start=g == 0, stop=False)
                    nc.tensor.matmul(o, ah, wol[:, g, :], start=False, stop=False)
                    last = nc.tensor.matmul(o, al, woh[:, g, :], start=False, stop=g == G - 1)
                return last

            for u in range(NK):
                c, half, kvl = u // 8, u % 8 // 4, u % 4
                if u == 0:
                    split(pe, 8)
                if u == 4:
                    split(pe, 12)
                if u == 8:
                    split(pe, 16)
                wait(pe, cos_done, u - 1)
                cs = slice(half * 512, (half + 1) * 512)
                three(prj[u % 2][:, :], [(wch[c][:, k, kvl * 128:(kvl + 1) * 128], wcl[c][:, k, kvl * 128:(kvl + 1) * 128],
                                          cth[:, k, cs], ctl[:, k, cs]) for k in range(KT)]).then_inc(proj_done, 1)
                if u == 0:
                    pe.wait_ge(masks, 1)
                    pe.wait_ge(consts, 1)
                    nc.tensor.matmul(trp[:, 0:S], ones[:, :], maskf[:, :], start=True, stop=True)\
                        .then_inc(mask_count, 1)
                if 6 <= u < 14:
                    i = u - 6
                    pe.wait_ge(xn_done, i + 1)
                    wait(pe, xt_lo, i)
                    if i == 0:
                        pe.wait_ge(masks, 2)
                        pe.wait_ge(tab_in, 16)
                    transpose4(trp, lambda k: nrm[:, i % 2, k * 128:(k + 1) * 128]).then_inc(xt_done, 1)
            for v in range(16):
                c, b = v // B, v % B
                if v % B == 0:
                    split(pe, 20 + 4 * c)
                wait(pe, v_copied, v - 1)
                bs = slice(b * 128, (b + 1) * 128)
                three(prj2[v % 2][:, :], [(cth[:, k, bs], ctl[:, k, bs], wch[c][:, k, :], wcl[c][:, k, :])
                                          for k in range(KT)]).then_inc(vproj_done, 1)
                g = first_query(v)
                if g is not None:
                    pe.wait_ge(xt_lo, 8)
                    split(pe, WQ0 + g + 1)
                    q_unit(NK + g, g, 0)

            def head(kv, first, last):
                for b in range(B):
                    j, h, s = 8 * kv + b, b // 4, b % 4
                    prev = not (first and b == 0)
                    if s == 0:
                        pe.wait_ge(roped, NK + 8 * kv + 4 * h + 4)
                        pe.wait_ge(k_in[h], 16 * kv + 16)
                    wait(pe, tanh_done, j)
                    nc.tensor.matmul(lgp[:, :], kcur[:, h, s * 128:(s + 1) * 128],
                                     qT[:, h, :, s * 128:(s + 1) * 128], start=True, stop=True)\
                        .then_inc(logits_done, 1)
                    if prev:
                        pe.wait_ge(an_done, j)
                        wait(pe, at_lo, j - 1)
                        transpose4(trp, lambda g: nrm[:, (b + 1) % 2, g * 128:(g + 1) * 128]).then_inc(at_done, 1)
                    if s in (0, 3):
                        for n in range(2):
                            slot = 2 + n if s == 0 else n
                            unit = j - 2 + n if s == 0 else j - 3 + n
                            if s == 0 and not prev:
                                continue
                            if s == 3 and h == 0 and n == 0:
                                split(pe, 8 * kv + WO0 + 4)
                            pe.wait_ge(at_lo, unit + 1)
                            wait(pe, y_done, unit - 1)
                            if n == 0:
                                out_mm(slot, range(G)).then_inc(out_done, 1)
                            else:
                                out_mm(slot, range(3))
                        if s == 0 and not prev:
                            pending = None
                        else:
                            pending = slot
                    else:
                        pending = None
                        if not (last and h == 1):
                            for n in range(2):
                                g = 2 * (s - 1) + n
                                if h == 1:
                                    split(pe, 8 * kv + 33 + g)
                                q_unit(8 * kv + NK + 4 * h + 4 + g, g, 1 - h)
                        elif s == 1:
                            token_transposes(0)
                            token_transposes(1)
                            weight_transposes(0)
                            weight_transposes(1)
                        else:
                            token_transposes(2)
                            token_transposes(3)
                    pe.wait_ge(weights_done, j + 1)
                    if s == 0:
                        pe.wait_ge(v_in[h], 16 * kv + 16)
                    wait(pe, an_done, j)
                    for g in range(G):
                        av = nc.tensor.matmul(avp[:, g // 2, (g % 2) * (DH + 1):(g % 2 + 1) * (DH + 1)],
                                              eb[:, b % 2, g * 128:(g + 1) * 128], vcur[:, b, :],
                                              start=True, stop=True)
                    av.then_inc(av_done, 1)
                    if pending is not None:
                        out_mm(pending, range(3, G)).then_inc(out_done, 1)

            def weight_transposes(n):
                pe.wait_ge(piece_in[n % 4], 16 * (STAGED + n // 4 + 1))
                if n < 2:
                    pe.wait_ge(y_done, NKV * B - 4)
                elif n == 2:
                    pe.wait_ge(at_lo, NKV * B)
                elif n == 3:
                    pe.wait_ge(tanh_done, NKV * B)
                else:
                    pe.wait_ge(wt_lo, n - 1)
                transpose4(wt_bank(n), lambda k: stage[:, n % 4, k * 128:(k + 1) * 128]).then_inc(wt_done, 1)

            def token_transposes(b):
                pe.wait_ge(xn_done, B + b + 1)
                if b < 2:
                    pe.wait_ge(cos_done, NK + 4 * 2 * NKV)
                elif b == 4:
                    pe.wait_ge(an_done, NKV * B)
                if b in (2, 3, 6, 7):
                    pe.wait_ge(xt_lo, B + b - 1)
                transpose4(xt_bank(b), lambda k: sw[:, b % 2, k * 128:(k + 1) * 128]).then_inc(xt_done, 1)

            steps_of_heads(pe, head)
            n_steps = NKV * B
            pe.wait_ge(an_done, n_steps)
            pe.wait_ge(at_lo, n_steps - 1)
            transpose4(trp, lambda g: nrm[:, 1, g * 128:(g + 1) * 128]).then_inc(at_done, 1)

            def last_out(unit):
                pe.wait_ge(at_lo, unit + 1)
                pe.wait_ge(y_done, unit - 1)
                out_mm(unit % 4, range(G)).then_inc(out_done, 1)

            def hidden(n, w):
                t, half = UNITS[n]
                cs = slice(half * 512, (half + 1) * 512)
                if w == 0:
                    pe.wait_ge(wt_lo, 2 * t + 2)
                    if n in (0, 2):
                        pe.wait_ge(xt_lo, B + 4 * (half + 1))
                    wait(pe, h_done, n - 1)
                return three((prj, prj2)[w][n % 2][:, :],
                             [(wgh[:, t % 2, w, k, :], wgl[:, t % 2, w, k, :], xh[:, k, cs], xl[:, k, cs])
                              for k in range(KT)])

            last_out(n_steps - 2)
            hidden(0, 0)
            weight_transposes(2)
            weight_transposes(3)
            last_out(n_steps - 1)
            token_transposes(4)
            token_transposes(5)
            pe.wait_ge(y_done, n_steps - 1)
            hidden(0, 1).then_inc(gate_done, 1)
            hidden(1, 0)
            token_transposes(6)
            token_transposes(7)
            pe.wait_ge(y_done, n_steps)
            hidden(1, 1).then_inc(gate_done, 1)
            weight_transposes(4)
            weight_transposes(5)
            for n in range(2, len(UNITS)):
                t, half = UNITS[n]
                if n > 3 and half == 0 and t < HT - 1:
                    weight_transposes(2 * t + 2)
                    weight_transposes(2 * t + 3)
                hidden(n, 0)
                hidden(n, 1).then_inc(gate_done, 1)

            def w3_transposes(n):
                m = 2 * HT + n
                p = 128 if n < HT - 1 else HLAST
                pe.wait_ge(piece_in[m % 4], 16 * (STAGED + m // 4 + 1))
                wait(pe, wt_lo, m - 1)
                transpose4(trg[m % 2], lambda i: stage[:, m % 4, i * 128:i * 128 + p], p).then_inc(wt_done, 1)

            def down(b, n, o):
                p = 128 if n < HT - 1 else HLAST
                ah, al = hh[0:p, n, b * 128:(b + 1) * 128], hl[0:p, n, b * 128:(b + 1) * 128]
                nc.tensor.matmul(o, ah, w3h[0:p, n, :], start=n == 0, stop=False)
                nc.tensor.matmul(o, ah, w3l[0:p, n, :], start=False, stop=False)
                return nc.tensor.matmul(o, al, w3h[0:p, n, :], start=False, stop=n == HT - 1)

            outs = [prj[0], prj[1], prj2[0], prj2[1]]
            w3_transposes(0)
            w3_transposes(1)
            for n in range(HT):
                pe.wait_ge(wt_lo, 2 * HT + n + 1)
                if n == 0:
                    pe.wait_ge(h_lo, 2 * HT)
                for b in range(4):
                    last = down(b, n, outs[b][:, :])
                    if n == HT - 1:
                        last.then_inc(down_done, 1)
                if n < HT - 2:
                    w3_transposes(n + 2)
            for b in range(4, B):
                pe.wait_ge(final_done, b - 3)
                for n in range(HT):
                    last = down(b, n, outs[b - 4][:, :])
                last.then_inc(down_done, 1)

        @block.scalar
        def _(act):
            def nf_above_bound(c, i):
                wait(act, nf_step, NF_STEPS * c + (4 if i < 2 else 3 + i))
                nc.scalar.activation(nfp[:, i % 2, :], nfv[:, :], ACT.Sign, bias=bnd[:, i:i + 1])\
                    .then_inc(nf_above, 1)

            def swap(ru, slot):
                act.wait_ge(proj_done, ru + 1)
                wait(act, roped, ru - 1)
                nc.scalar.activation(sw[0:64, slot, :], prj[slot][64:128, :], ACT.Copy)
                nc.scalar.activation(sw[64:128, slot, :], prj[slot][0:64, :], ACT.Copy).then_inc(swapped, 1)

            for u in range(NK):
                swap(u, u % 2)
                if 6 <= u < 14:
                    i = u - 6
                    act.wait_ge(xt_done, i + 1)
                    nc.scalar.activation(xh[:, :, i * 128:(i + 1) * 128],
                                         trp[:, :].rearrange("p (k t) -> p k t", k=KT), ACT.Copy).then_inc(xt_hi, 1)
                if u == 0:
                    act.wait_ge(consts, 3)
                for i in nf_keys(u):
                    nf_above_bound(0, i)
            for v in range(16):
                act.wait_ge(vproj_done, v + 1)
                wait(act, v_out[v % 4], 16 * (v // 4))
                nc.scalar.activation(vst[:, v % 4, :], prj2[v % 2][:, :], ACT.Copy).then_inc(v_copied, 1)
                chunk, bounds = nf_values(v)
                for i in bounds[0:1]:
                    nf_above_bound(chunk, i)
                g = first_query(v)
                if g is not None:
                    swap(NK + g, g % 2)
                for i in bounds[1:]:
                    nf_above_bound(chunk, i)

            def head(kv, first, last):
                for b in range(B):
                    j, h, s = 8 * kv + b, b // 4, b % 4
                    act.wait_ge(logits_done, j + 1)
                    wait(act, av_done, j - 1)
                    nc.scalar.activation(eb[:, b % 2, :], lgp[:, :], ACT.Tanh, scale=MULT / CAP).then_inc(tanh_done, 1)
                    act.wait_ge(tanh_done, j + 1)
                    nc.scalar.activation(eb[:, b % 2, :], eb[:, b % 2, :], ACT.Exp, scale=CAP).then_inc(exp_done, 1)
                    if not (first and b == 0):
                        act.wait_ge(at_done, j)
                        wait(act, out_done, j - 4)
                        nc.scalar.activation(ath[:, (b + 3) % 4, :], trp[:, :], ACT.Copy).then_inc(at_hi, 1)
                    for i in nf_head(b)[0:1]:
                        nf_above_bound(kv + 2, i)
                    if s in (1, 2) and not (last and h == 1):
                        swap(8 * kv + NK + 4 * h + 4 + 2 * (s - 1), 0)
                    for i in nf_head(b)[1:]:
                        nf_above_bound(kv + 2, i)
                    if s in (1, 2) and not (last and h == 1):
                        swap(8 * kv + NK + 4 * h + 5 + 2 * (s - 1), 1)
                    if last and b == 5:
                        token_hi(0)
                        token_hi(1)
                        weight_hi(0)
                        weight_hi(1)
                    if last and b == 6:
                        token_hi(2)
                        token_hi(3)

            def weight_hi(n):
                act.wait_ge(wt_done, n + 1)
                if n >= 4:
                    act.wait_ge(gate_done, units_of(n // 2 - 2))
                nc.scalar.activation(wgh[:, n // 2 % 2, n % 2, :, :],
                                     wt_bank(n)[:, :].rearrange("p (k h) -> p k h", k=KT), ACT.Copy).then_inc(wt_hi, 1)

            def token_hi(b):
                act.wait_ge(xt_done, B + b + 1)
                nc.scalar.activation(xh[:, :, b * 128:(b + 1) * 128],
                                     xt_bank(b).rearrange("p (k t) -> p k t", k=KT), ACT.Copy).then_inc(xt_hi, 1)

            def silu(n):
                act.wait_ge(gate_done, n + 1)
                wait(act, h_done, n - 1)
                nc.scalar.activation(sg[:, n % 2, :], prj[n % 2][:, :], ACT.Silu).then_inc(silu_done, 1)

            steps_of_heads(act, head)
            n_steps = NKV * B
            act.wait_ge(at_done, n_steps)
            act.wait_ge(out_done, n_steps - 4)
            nc.scalar.activation(ath[:, 3, :], trp[:, :], ACT.Copy).then_inc(at_hi, 1)
            weight_hi(2)
            weight_hi(3)
            token_hi(4)
            token_hi(5)

            for n in range(len(UNITS)):
                t, half = UNITS[n]
                if n == 1:
                    token_hi(6)
                    token_hi(7)
                if n == 3:
                    weight_hi(4)
                    weight_hi(5)
                if n > 3 and half == 0 and t < HT - 1:
                    weight_hi(2 * t + 2)
                    weight_hi(2 * t + 3)
                silu(n)
                chunk, bounds = nf_ffn(n)
                for i in bounds:
                    nf_above_bound(chunk, i)
            for n in range(HT):
                m = 2 * HT + n
                p = 128 if n < HT - 1 else HLAST
                act.wait_ge(wt_done, m + 1)
                if n == 0:
                    act.wait_ge(gate_done, 2 * HT)
                nc.scalar.activation(w3h[0:p, n, :].rearrange("h (a r q) -> h a q r", a=2, q=2),
                                     trg[m % 2][0:p, :].rearrange("h (a q r) -> h a q r", a=2, q=2), ACT.Copy)\
                    .then_inc(wt_hi, 1)

        @block.vector
        def _(dve):
            def as_f32(ap):
                return ap.bitcast(f32)

            def batches(table):
                return table.rearrange("p (o t) -> p o t", o=1).to_broadcast([128, 4, S])

            def blocks(ap):
                return ap.rearrange("p (b e) -> p b e", e=BLK)

            def spread(ap):
                return ap.rearrange("p (b o) -> p b o", o=1).to_broadcast([128, CH // BLK, BLK])

            def nf(c, i):
                if i == 0:
                    dve.wait_ge(nf_in, 16 * c + 16)
                if i > 0 or not isinstance(c, int) or c > 0:
                    dve.wait_ge(nf_step, NF_STEPS * c + i)
                if i == 0:
                    op = nc.vector.tensor_reduce(nfm[:, :], blocks(nfv[:, :]), axis=AX.X, op=ALU.max,
                                                 apply_absolute_value=True)
                elif i == 1:
                    op = nc.vector.scalar_tensor_tensor(nfg[:, :], nfm[:, :], 0.0, nfm[:, :], ALU.is_equal, ALU.add)
                elif i == 2:
                    op = nc.vector.reciprocal(nfr[:, :], nfg[:, :])
                elif i == 3:
                    op = nc.vector.tensor_tensor(blocks(nfv[:, :]), blocks(nfv[:, :]), spread(nfr[:, :]), ALU.mult)
                elif i < 19:
                    b = i - 4
                    dve.wait_ge(nf_above, 15 * c + b + 1)
                    if b == 0:
                        if not isinstance(c, int) or c > 0:
                            dve.wait_ge(nf_out, 16 * c)
                        op = nc.vector.tensor_scalar(nfa[:, :], nfp[:, 0, :], STEPS[0], NF4_CODE[0], ALU.mult, ALU.add)
                    else:
                        op = nc.vector.scalar_tensor_tensor(nfa[:, :], nfp[:, b % 2, :], STEPS[b], nfa[:, :],
                                                            ALU.mult, ALU.add)
                else:
                    op = nc.vector.tensor_tensor(blocks(nfa[:, :]), blocks(nfa[:, :]), spread(nfm[:, :]), ALU.mult)
                op.then_inc(nf_step, 1)

            def piece(slot, rounds, hi):
                dve.wait_ge(piece_in[slot], 16 * rounds)
                nc.vector.tensor_copy(hi, stage[:, slot, :]).then_inc(piece_hi, 1)

            def cos_part(ru, slot, dst, cos):
                dve.wait_ge(swapped, ru + 1)
                nc.vector.tensor_tensor(dst.rearrange("p (b t) -> p b t", b=4),
                                        prj[slot][:, :].rearrange("p (b t) -> p b t", b=4), batches(cos), ALU.mult)\
                    .then_inc(cos_done, 1)

            nc.vector.memset(ones[:, :], 1.0).then_inc(consts, 1)
            nc.vector.memset(vcur[:, :, :], 1.0).then_inc(consts, 1)
            for i in range(15):
                last = nc.vector.memset(bnd[:, i:i + 1], -BOUNDS[i])
            last.then_inc(consts, 1)
            nc.vector.memset(half_neg[:, :], -0.5).then_inc(consts, 1)
            def first_piece(n):
                src, arrived, value = source(n)
                hi, lo = parts(n)
                if n == 16:
                    dve.wait_ge(proj_done, 8)
                if n == 20:
                    dve.wait_ge(proj_done, 16)
                dve.wait_ge(arrived, value)
                nc.vector.tensor_copy(hi, src).then_inc(piece_hi, 1)
                if n % 2:
                    dve.wait_ge(piece_hi, n + 1)
                    nc.vector.tensor_tensor(lo, src, as_f32(hi), ALU.subtract).then_inc(piece_lo_dve, 1)

            for n in range(12):
                first_piece(n)
            dve.wait_ge(mask_in, 16)
            nc.vector.tensor_copy(maskf[:, :], mt8[:, :]).then_inc(masks, 1)
            dve.wait_ge(mask_count, 1)
            dve.wait_ge(tab_in, 16)
            nc.vector.tensor_scalar(nomask[:, :], trp[:, 0:S], 0.5, None, ALU.is_lt).then_inc(mask_step, 1)
            nc.vector.tensor_scalar(keep[:, :], trp[:, 0:S], 0.5, None, ALU.is_gt).then_inc(mask_step, 1)
            dve.wait_ge(mask_step, 2)
            nc.vector.tensor_tensor(maskf[:, :], maskf[:, :], nomask[:, :], ALU.add)
            nc.vector.tensor_tensor(cosq[:, :], tab[:, 0, :], keep[:, :], ALU.mult)
            nc.vector.tensor_tensor(sinq[:, :], tab[:, 1, :], keep[:, :], ALU.mult).then_inc(masks, 1)

            def ln_moments(k, tokens, ahead=0):
                for b in tokens[ahead:]:
                    last = nc.vector.bn_stats(stat[:, b, :], y[:, b, :])
                last.then_inc(ln_step, 1)
                dve.wait_ge(ln_step, 6 * k + 1)
                for b in tokens:
                    last = nc.vector.bn_aggr(mv[:, b, :], stat[:, b, :])
                last.then_inc(ln_step, 1)
                dve.wait_ge(ln_step, 6 * k + 2)
                bs = slice(tokens[0], tokens[-1] + 1)
                nc.vector.tensor_scalar(veps[:, bs], mv[:, bs, 1], EPS, None, ALU.add).then_inc(ln_var, 1)

            def ln_rstd(k, tokens):
                bs = slice(tokens[0], tokens[-1] + 1)
                dve.wait_ge(ln_guess, k + 1)
                nc.vector.tensor_tensor(corr[:, bs], guess[:, bs], guess[:, bs], ALU.mult).then_inc(ln_step, 1)
                dve.wait_ge(ln_step, 6 * k + 3)
                nc.vector.tensor_tensor(corr[:, bs], corr[:, bs], veps[:, bs], ALU.mult).then_inc(ln_step, 1)
                dve.wait_ge(ln_step, 6 * k + 4)
                nc.vector.tensor_scalar(corr[:, bs], corr[:, bs], -0.5, 1.5, ALU.mult, ALU.add).then_inc(ln_step, 1)
                dve.wait_ge(ln_step, 6 * k + 5)
                nc.vector.tensor_tensor(rstd[:, bs], guess[:, bs], corr[:, bs], ALU.mult).then_inc(ln_step, 1)
                dve.wait_ge(ln_step, 6 * k + 6)

            def ln_stats(k, tokens):
                ln_moments(k, tokens)
                ln_rstd(k, tokens)

            def normalise(b, to):
                nc.vector.tensor_scalar(to[:, b % 2, :], y[:, b, :], mv[:, b, 0:1], rstd[:, b:b + 1],
                                        ALU.subtract, ALU.mult).then_inc(xn_done, 1)

            def token_lo(b, round, src):
                dve.wait_ge(xt_hi, 8 * round + b + 1)
                ts = slice(b * 128, (b + 1) * 128)
                nc.vector.tensor_tensor(xl[:, :, ts], src.rearrange("p (k t) -> p k t", k=KT),
                                        as_f32(xh[:, :, ts]), ALU.subtract).then_inc(xt_lo, 1)

            for n in range(12, 16):
                first_piece(n)
            for u in range(NK):
                if u >= 8:
                    dve.wait_ge(k_out[u - 8], 16)
                cos_part(u, u % 2, qT[:, u % 8 // 4, u % 4, :], tab[:, 0, :])
                if u == 1:
                    dve.wait_ge(x_in, 16)
                    for b in range(4):
                        nc.vector.bn_stats(stat[:, b, :], y[:, b, :])
                if u == 2:
                    ln_moments(0, range(B), 4)
                if u == 3:
                    ln_rstd(0, range(B))
                    normalise(0, nrm)
                    normalise(1, nrm)
                if 6 <= u < 14:
                    i = u - 6
                    token_lo(i, 0, trp[:, :])
                    if i + 2 < B:
                        dve.wait_ge(xt_done, i + 1)
                        normalise(i + 2, nrm)
                if 8 <= u < 12:
                    first_piece(u + 8)
                if u == 4:
                    for i in range(4):
                        nf(0, i)
                for i in nf_keys(u):
                    nf(0, 4 + i)
            for n in range(20, 24):
                first_piece(n)
            for v in range(16):
                if v < 4:
                    first_piece(24 + v)
                if v == 6:
                    for i in range(3):
                        nf(1, i)
                chunk, bounds = nf_values(v)
                for i in bounds[0:1]:
                    nf(chunk, 4 + i)
                g = first_query(v)
                if g is not None:
                    dve.wait_ge(k_out[g], 32)
                    cos_part(NK + g, g % 2, qT[:, 0, g, :], cosq[:, :])
                for i in bounds[1:]:
                    nf(chunk, 4 + i)

            def head(kv, first, last):
                for b in range(B):
                    j, h, s = 8 * kv + b, b // 4, b % 4
                    prev = not (first and b == 0)
                    if prev:
                        dve.wait_ge(at_hi, j)
                        nc.vector.tensor_tensor(atl[:, (b + 3) % 4, :], trp[:, :], as_f32(ath[:, (b + 3) % 4, :]),
                                                ALU.subtract).then_inc(at_lo, 1)
                    for n in range(2):
                        if b in (1, 2):
                            g = 2 * (b - 1) + n
                            if g == 0:
                                wait(dve, out_done, 8 * kv)
                                if first:
                                    dve.wait_ge(vproj_done, 16)
                            piece(g, 2 * kv + 6, woh[:, g, :])
                        if b in (3, 4) and not last:
                            g = 2 * (b - 3) + n
                            if g == 0:
                                dve.wait_ge(proj_done, 8 * kv + NK + 8)
                            piece(g, 2 * kv + 7, wqh[:, g, :, :].rearrange("p k n -> p (k n)"))
                    for i in nf_head(b)[0:1]:
                        nf(kv + 2, 4 + i)
                    if b == 0:
                        for i in range(3):
                            nf(kv + 2, i)

                    def project(n):
                        if s in (0, 3):
                            if s == 0 and not prev:
                                return
                            unit = j - 2 + n if s == 0 else j - 3 + n
                            batch = (b - 2 + n) % 8 if s == 0 else b - 3 + n
                            dve.wait_ge(out_done, unit + 1)
                            nc.vector.tensor_tensor(y[:, batch, :], prj2[n][:, :], y[:, batch, :], ALU.add)\
                                .then_inc(y_done, 1)
                        elif not (last and h == 1):
                            g = 2 * (s - 1) + n
                            cos_part(8 * kv + NK + 4 * h + 4 + g, g % 2, qT[:, 1 - h, g, :], cosq[:, :])

                    if last and b == 4:
                        dve.wait_ge(y_done, NKV * B - 6)
                        ln_stats(1, range(0, 2))
                        normalise(0, sw)
                        normalise(1, sw)
                    if last and b == 5:
                        dve.wait_ge(y_done, NKV * B - 4)
                        ln_stats(2, range(2, 4))
                        for i in range(2):
                            token_lo(i, 1, xt_bank(i))
                            dve.wait_ge(xt_done, B + i + 1)
                            normalise(i + 2, sw)
                    if last and b == 6:
                        token_lo(2, 1, xt_bank(2))
                        token_lo(3, 1, xt_bank(3))
                    project(0)
                    dve.wait_ge(av_done, j + 1)
                    nc.vector.reciprocal(rs[:, :].rearrange("p (a c) -> p a c", a=2),
                                         avp[:, :, DH:2 * (DH + 1):DH + 1]).then_inc(recip_done, 1)
                    dve.wait_ge(recip_done, j + 1)
                    nc.vector.tensor_tensor(
                        nrm[:, b % 2, :].rearrange("p (a c d) -> p a c d", a=2, c=2),
                        avp[:, :, 0:2 * (DH + 1)].rearrange("p a (c d) -> p a c d", c=2)[:, :, :, 0:DH],
                        rs[:, :].rearrange("p (a c o) -> p a c o", a=2, c=2).to_broadcast([128, 2, 2, DH]),
                        ALU.mult).then_inc(an_done, 1)
                    for i in nf_head(b)[1:]:
                        nf(kv + 2, 4 + i)
                    project(1)
                    if last and b == 5:
                        weight_lo(0)
                        weight_lo(1)

            def weight_lo(n):
                dve.wait_ge(wt_hi, n + 1)
                nc.vector.tensor_tensor(wgl[:, n // 2 % 2, n % 2, :, :],
                                        wt_bank(n)[:, :].rearrange("p (k h) -> p k h", k=KT),
                                        as_f32(wgh[:, n // 2 % 2, n % 2, :, :]), ALU.subtract).then_inc(wt_lo, 1)

            def last_y(unit):
                dve.wait_ge(out_done, unit + 1)
                nc.vector.tensor_tensor(y[:, unit % 8, :], prj2[unit % 2][:, :], y[:, unit % 8, :], ALU.add)\
                    .then_inc(y_done, 1)

            steps_of_heads(dve, head)
            n_steps = NKV * B
            dve.wait_ge(at_hi, n_steps)
            nc.vector.tensor_tensor(atl[:, 3, :], trp[:, :], as_f32(ath[:, 3, :]), ALU.subtract).then_inc(at_lo, 1)
            last_y(n_steps - 2)
            dve.wait_ge(y_done, n_steps - 1)
            ln_stats(3, range(4, 6))
            normalise(4, sw)
            normalise(5, sw)
            weight_lo(2)
            weight_lo(3)
            last_y(n_steps - 1)

            dve.wait_ge(y_done, n_steps)
            ln_stats(4, range(6, B))
            for b in range(4, 6):
                token_lo(b, 1, xt_bank(b))
                normalise(b + 2, sw)

            def hidden(n):
                t, half = UNITS[n]
                dve.wait_ge(silu_done, n + 1)
                wait(dve, h_lo, n - 1)
                nc.vector.tensor_tensor(hf[:, n % 2, :], prj2[n % 2][:, :], sg[:, n % 2, :], ALU.mult)\
                    .then_inc(h_done, 1)
                dve.wait_ge(h_done, n + 1)
                nc.vector.tensor_copy(hh[:, t, half * 512:(half + 1) * 512], hf[:, n % 2, :]).then_inc(h_hi, 1)

            for n in range(len(UNITS)):
                t, half = UNITS[n]
                if n == 1:
                    token_lo(6, 1, xt_bank(6))
                    token_lo(7, 1, xt_bank(7))
                if n == 3:
                    weight_lo(4)
                    weight_lo(5)
                if n > 3 and half == 0 and t < HT - 1:
                    weight_lo(2 * t + 2)
                    weight_lo(2 * t + 3)
                hidden(n)
                if n in (1, 10):
                    for i in range(3):
                        nf(10 + n // 10, i)
                chunk, bounds = nf_ffn(n)
                for i in bounds:
                    nf(chunk, 4 + i)
            for n in range(HT):
                m = 2 * HT + n
                p = 128 if n < HT - 1 else HLAST
                dve.wait_ge(wt_hi, m + 1)
                nc.vector.tensor_tensor(w3l[0:p, n, :].rearrange("h (a r q) -> h a q r", a=2, q=2),
                                        trg[m % 2][0:p, :].rearrange("h (a q r) -> h a q r", a=2, q=2),
                                        as_f32(w3h[0:p, n, :]).rearrange("h (a r q) -> h a q r", a=2, q=2),
                                        ALU.subtract).then_inc(wt_lo, 1)
            outs = [prj[0], prj[1], prj2[0], prj2[1]]
            for b in range(B):
                dve.wait_ge(down_done, b + 1)
                nc.vector.tensor_tensor(y[:, b, :], outs[b % 4][:, :], y[:, b, :], ALU.add).then_inc(final_done, 1)

        @block.gpsimd
        def _(pool):
            def low(slot, hi, lo, n):
                pool.wait_ge(piece_hi, n + 1)
                nc.gpsimd.tensor_tensor(lo, stage[:, slot, :], hi.bitcast(f32), ALU.subtract).then_inc(piece_lo, 1)

            def flat(ap):
                return ap.rearrange("p k n -> p (k n)")

            def rope(ru, slot, dst, sin):
                pool.wait_ge(swapped, ru + 1)
                part = sw[:, slot, :].rearrange("p (b t) -> p b t", b=4)
                nc.gpsimd.tensor_tensor(part, part, sin.rearrange("p (o t) -> p o t", o=1).to_broadcast([128, 4, S]),
                                        ALU.mult).then_inc(sin_done, 1)
                pool.wait_ge(cos_done, ru + 1)
                pool.wait_ge(sin_done, ru + 1)
                nc.gpsimd.tensor_tensor(dst, dst, sw[:, slot, :], ALU.add).then_inc(roped, 1)

            def first_low(n):
                pool.wait_ge(piece_hi, n + 1)
                hi, lo = parts(n)
                nc.gpsimd.tensor_tensor(lo, source(n)[0], hi.bitcast(f32), ALU.subtract).then_inc(piece_lo, 1)

            def power(k, tokens):
                pool.wait_ge(ln_var, k + 1)
                bs = slice(tokens[0], tokens[-1] + 1)
                nc.gpsimd.tensor_tensor(guess[:, bs], veps[:, bs], half_neg[:, bs], ALU.pow).then_inc(ln_guess, 1)

            def nf_scale(c, i, what, by):
                pool.wait_ge(nf_step, NF_STEPS * c + i)
                blocks = what[:, :].rearrange("p (b e) -> p b e", e=BLK)
                nc.gpsimd.tensor_tensor(blocks, blocks, by[:, :].rearrange("p (b o) -> p b o", o=1)
                                        .to_broadcast([128, CH // BLK, BLK]), ALU.mult).then_inc(nf_step, 1)

            for n in range(0, 16, 2):
                first_low(n)
            pool.wait_ge(tab_in, 16)
            for u in range(NK):
                rope(u, u % 2, qT[:, u % 8 // 4, u % 4, :], tab[:, 1, :])
                if u == 2:
                    power(0, range(B))
                if u in (8, 10):
                    first_low(u + 8)
            for n in range(20, 28, 2):
                first_low(n)
            nf_scale(0, 19, nfa, nfm)
            nf_scale(1, 3, nfv, nfr)
            pool.wait_ge(masks, 2)
            for g in range(G):
                rope(NK + g, g % 2, qT[:, 0, g, :], sinq[:, :])
            nf_scale(1, 19, nfa, nfm)

            def head(kv, first, last):
                for b in range(B):
                    j, h, s = 8 * kv + b, b // 4, b % 4
                    pool.wait_ge(exp_done, j + 1)
                    part = eb[:, b % 2, :].rearrange("p (g t) -> p g t", g=G)
                    nc.gpsimd.tensor_tensor(part, part,
                                            maskf[:, :].rearrange("p (o t) -> p o t", o=1).to_broadcast([128, G, S]),
                                            ALU.mult).then_inc(weights_done, 1)
                    for n in range(2):
                        if b in (1, 2):
                            g = 2 * (b - 1) + n
                            low(g, woh[:, g, :], wol[:, g, :], 8 * kv + WO0 + g)
                        if b in (3, 4) and not last:
                            g = 2 * (b - 3) + n
                            low(g, flat(wqh[:, g, :, :]), flat(wql[:, g, :, :]), 8 * kv + 32 + g)
                    if s in (1, 2) and not (last and h == 1):
                        for n in range(2):
                            g = 2 * (s - 1) + n
                            rope(8 * kv + NK + 4 * h + 4 + g, g % 2, qT[:, 1 - h, g, :], sinq[:, :])
                    if last and b == 4:
                        power(1, range(0, 2))
                    if last and b == 5:
                        power(2, range(2, 4))
                    if b == 0:
                        nf_scale(kv + 2, 3, nfv, nfr)
                nf_scale(kv + 2, 19, nfa, nfm)

            steps_of_heads(pool, head)
            power(3, range(4, 6))
            power(4, range(6, B))
            for n, (t, half) in enumerate(UNITS):
                cs = slice(half * 512, (half + 1) * 512)
                pool.wait_ge(h_hi, n + 1)
                nc.gpsimd.tensor_tensor(hl[:, t, cs], hf[:, n % 2, :], hh[:, t, cs].bitcast(f32), ALU.subtract)\
                    .then_inc(h_lo, 1)
                if n in (1, 10):
                    nf_scale(10 + n // 10, 3, nfv, nfr)
                if n in (9, 18):
                    nf_scale(10 + n // 18, 19, nfa, nfm)


def kernel(x, ctx_4096, mask_1x1xSxS2_bk0, L0_xattn_Wq, L0_xattn_Wk, L0_xattn_Wv, L0_xattn_Wo,
           L0_ffn_w1, L0_ffn_w2, L0_ffn_w3):
    import concourse.bacc as bacc
    from concourse.bass_utils import run_bass_kernel_spmd

    f = np.ascontiguousarray
    x, ctx_ = np.asarray(x), np.asarray(ctx_4096)
    ct = ctx_.reshape(TOK, D).T.reshape(KT, 128, 2, 512).transpose(2, 0, 1, 3).reshape(8, 128, 512)
    wk = np.asarray(L0_xattn_Wk).reshape(KT, 128, 2, 512).transpose(2, 0, 1, 3).reshape(8, 128, 512)
    wv = np.asarray(L0_xattn_Wv).reshape(KT, 128, 2, 512).transpose(2, 0, 1, 3).reshape(8, 128, 512)
    wq = np.asarray(L0_xattn_Wq).reshape(KT, 128, NQ, 128).transpose(2, 1, 0, 3).reshape(NQ, 128, 512)
    wo = np.asarray(L0_xattn_Wo).reshape(NQ, 128, D)
    w1, w2, w3 = (np.asarray(w) for w in (L0_ffn_w1, L0_ffn_w2, L0_ffn_w3))
    parts = [np.pad(w, ((0, HT * 128 - HID), (0, 0))).reshape(HT, 128, D).transpose(1, 0, 2).reshape(128, NFW)
             for w in (w1, w2)]
    parts.append(np.pad(w3.reshape(2, 128, 2 * HID).transpose(1, 0, 2).reshape(128, 4 * HID),
                        ((0, 0), (0, NFW - 4 * HID))))
    nf = np.split(np.concatenate(parts, axis=1), 12, axis=1)
    nf_first, nf_rest = (np.concatenate([nf[c] for c in cs], axis=1) for cs in ([8, 9, 0, 10, 11], range(1, 8)))
    mask = f(np.asarray(mask_1x1xSxS2_bk0)[0, 0].T)
    inv = (np.float32(1.0) / np.float32(10000.0) ** (np.arange(0, DH, 2, dtype=np.float32) / np.float32(DH))).astype(np.float32)
    phase = np.tile(np.arange(S, dtype=np.float32)[None, :] * inv[:, None], (2, 1)).astype(np.float32)
    sign = np.where(np.arange(DH) < DH // 2, -1.0, 1.0)[:, None]
    table = np.stack([np.cos(phase), sign * np.sin(phase), np.eye(128)], axis=1).astype(np.float32)

    nc = bacc.Bacc("TRN2", target_bir_lowering=False, num_devices=1)
    arrays = {"x_in": f(x), "ctx_pieces": f(ct), "wk_pieces": f(wk), "wv_pieces": f(wv), "wq_pieces": f(wq),
              "wo_pieces": f(wo), "nf_first": f(nf_first), "nf_rest": f(nf_rest), "mask_t": mask, "tables": table}
    args = [nc.dram_tensor(name, a.shape, mybir.dt.from_np(a.dtype), kind="ExternalInput").ap()
            for name, a in arrays.items()]
    out = nc.dram_tensor("out", (B, S, D), mybir.dt.float32, kind="ExternalOutput").ap()
    build(nc, *args, out)
    r = run_bass_kernel_spmd(nc, [arrays], core_ids=[0])
    return r.results[0]["out"]
```
